# Optimizing a Trainium2 kernel written in Bass

```python
import numpy as np
import jax
import jax.numpy as jnp

def _softmax(x, axis=-1):
    return jax.nn.softmax(x, axis=axis)

def _gelu(x):
    return jax.nn.gelu(x, approximate=True)

def _silu(x):
    return jax.nn.silu(x)

def _sigmoid(x):
    return jax.nn.sigmoid(x)

def _layernorm(x, axis=-1, eps=1e-05):
    m = jnp.mean(x, axis=axis, keepdims=True)
    v = jnp.var(x, axis=axis, keepdims=True)
    return (x - m) / jnp.sqrt(v + eps)

def _scatter_add(tgt, idx, src, axis=0):
    return tgt.at[idx].add(src)

def _segment_sum(src, seg, n):
    return jax.ops.segment_sum(src, seg, n)
kernel_name = 'mk_adaln_d1_jaxref_r8_b23a58'

def setup_inputs(seed: int=0):
    np.random.seed(seed)
    _w = jnp.asarray

    def _L0_attn_setup():
        import jax, jax.numpy as jnp
        import numpy as np
        DIM = 128
        HID = 192
        K = 4
        N, T = (4, 512)

        def _mk_forget_base(h, a=0.001, b=0.1, lo=-4.323, hi=-9.0):
            x = np.log(np.expm1(np.linspace(a, b, h, dtype=np.float64)))
            x = (x - x.min()) / (x.max() - x.min())
            x = x * abs(hi - lo) + hi
            return jnp.asarray(x, dtype=jnp.float32)
        key = jax.random.key(seed)
        ks = jax.random.split(key, 6)
        x = jax.random.normal(ks[0], (N, T, DIM), jnp.float32)
        Wi = jax.random.normal(ks[1], (2 * HID, DIM), jnp.float32) * DIM ** (-0.5)
        conv_w = jax.random.normal(ks[2], (HID, 1, K), jnp.float32) * K ** (-0.5)
        conv_b = jax.random.normal(ks[3], (HID,), jnp.float32) * 0.01
        Wg = jax.random.normal(ks[4], (2 * HID, HID), jnp.float32) * HID ** (-0.5)
        bg = jnp.zeros((2 * HID,), jnp.float32)
        forget_base = _mk_forget_base(HID)
        Wo = jax.random.normal(ks[5], (DIM, HID), jnp.float32) * HID ** (-0.5)
        return {'x': x, 'Wi': Wi, 'conv_w': conv_w, 'conv_b': conv_b, 'Wg': Wg, 'bg': bg, 'forget_base': forget_base, 'Wo': Wo}
    _L0_attn_in = _L0_attn_setup()

    def _L0_ffn_setup():
        import jax, jax.numpy as jnp
        import numpy as np
        B, S, D, F, E = (8, 128, 128, 512, 8)
        EPS = 1e-05
        key = jax.random.key(seed)
        ks = jax.random.split(key, 4)
        s = 0.02
        return {'input_features': jax.random.normal(ks[0], (B, S, D), jnp.float32), 'centroids': jax.random.normal(ks[1], (E, D), jnp.float32) * 0.1, 'ln_g': jnp.ones((E, D), jnp.float32), 'ln_b': jnp.zeros((E, D), jnp.float32), 'w1': jax.random.normal(ks[2], (E, D, F), jnp.float32) * s, 'b1': jnp.zeros((E, F), jnp.float32), 'w2': jax.random.normal(ks[3], (E, F, D), jnp.float32) * s, 'b2': jnp.zeros((E, D), jnp.float32)}
    _L0_ffn_in = _L0_ffn_setup()
    _L0_c = _w((lambda *s: np.random.randn(*s).astype(np.float32) * 0.05)(2, 128))
    _L0_wmod = _w((lambda *s: np.random.randn(*s).astype(np.float32) * 0.05)(128, 6 * 128) * 128 ** (-0.5))
    _d = {'L0_attn_x': _L0_attn_in['x'], 'L0_attn_Wi': _L0_attn_in['Wi'], 'L0_attn_conv_w': _L0_attn_in['conv_w'], 'L0_attn_conv_b': _L0_attn_in['conv_b'], 'L0_attn_Wg': _L0_attn_in['Wg'], 'L0_attn_bg': _L0_attn_in['bg'], 'L0_attn_forget_base': _L0_attn_in['forget_base'], 'L0_attn_Wo': _L0_attn_in['Wo'], 'L0_ffn_centroids': _L0_ffn_in['centroids'], 'L0_ffn_ln_g': _L0_ffn_in['ln_g'], 'L0_ffn_ln_b': _L0_ffn_in['ln_b'], 'L0_ffn_w1': _L0_ffn_in['w1'], 'L0_ffn_b1': _L0_ffn_in['b1'], 'L0_ffn_w2': _L0_ffn_in['w2'], 'L0_ffn_b2': _L0_ffn_in['b2'], 'L0_c': _L0_c, 'L0_wmod': _L0_wmod}
    _x0 = _d['L0_attn_x']
    _d['L0_attn_x'] = jax.random.normal(jax.random.fold_in(jax.random.key(seed), 1), (2, 2048, 128), dtype=_x0.dtype)
    del _x0
    return _d

def reference(L0_attn_x, L0_attn_Wi, L0_attn_conv_w, L0_attn_conv_b, L0_attn_Wg, L0_attn_bg, L0_attn_forget_base, L0_attn_Wo, L0_ffn_centroids, L0_ffn_ln_g, L0_ffn_ln_b, L0_ffn_w1, L0_ffn_b1, L0_ffn_w2, L0_ffn_b2, L0_c, L0_wmod):

    def _L0_attn_ref(x, Wi, conv_w, conv_b, Wg, bg, forget_base, Wo):
        import jax, jax.numpy as jnp
        import numpy as np
        DIM = 128
        HID = 192
        K = 4
        N, T = (4, 512)

        def _mk_forget_base(h, a=0.001, b=0.1, lo=-4.323, hi=-9.0):
            x = np.log(np.expm1(np.linspace(a, b, h, dtype=np.float64)))
            x = (x - x.min()) / (x.max() - x.min())
            x = x * abs(hi - lo) + hi
            return jnp.asarray(x, dtype=jnp.float32)
        gi = jnp.einsum('ntc,hc->nth', x, Wi)
        gate, u = jnp.split(gi, 2, axis=-1)
        u = jax.lax.conv_general_dilated(u.transpose(0, 2, 1), conv_w, window_strides=(1,), padding=[(K - 1, 0)], dimension_numbers=('NCH', 'OIH', 'NCH'), feature_group_count=HID) + conv_b[None, :, None]
        u = u.transpose(0, 2, 1)
        fg = jnp.einsum('nth,gh->ntg', u, Wg) + bg
        forget, inp = jnp.split(fg, 2, axis=-1)
        alpha = jnp.exp(-8.0 * jax.nn.softplus(forget_base) * jax.nn.sigmoid(forget))
        beta = jnp.sqrt(1.0 - alpha ** 2 + 1e-06)
        xt = beta * jax.nn.sigmoid(inp) * u

        def step(h, ax):
            a, xx = ax
            h = a * h + xx
            return (h, h)
        _, h = jax.lax.scan(step, jnp.zeros((x.shape[0], HID), x.dtype), (alpha.transpose(1, 0, 2), xt.transpose(1, 0, 2)))
        h = h.transpose(1, 0, 2)
        return jnp.einsum('nth,ch->ntc', jax.nn.gelu(gate, approximate=False) * h, Wo)

    def _L0_ffn_ref(input_features, centroids, ln_g, ln_b, w1, b1, w2, b2):
        import jax, jax.numpy as jnp
        import numpy as np
        B, S, D, F, E = (8, 128, 128, 512, 8)
        EPS = 1e-05
        x = input_features.reshape(-1, D)
        aff = jax.lax.stop_gradient(x @ centroids.T)
        eid = jnp.argmax(aff, axis=-1)
        alpha = jax.nn.sigmoid(jnp.sum(x * centroids[eid], axis=-1, keepdims=True))
        mu = jnp.mean(x, axis=-1, keepdims=True)
        var = jnp.mean((x - mu) ** 2, axis=-1, keepdims=True)
        xn = (x - mu) * jax.lax.rsqrt(var + EPS)
        xln = xn * ln_g[eid] + ln_b[eid]
        onehot = jax.nn.one_hot(eid, E, dtype=x.dtype)
        ffn = jnp.zeros_like(x)
        for e in range(E):
            h = jax.nn.relu(xln @ w1[e] + b1[e])
            ffn = ffn + onehot[:, e:e + 1] * (h @ w2[e] + b2[e])
        out = x + alpha * ffn
        return out.reshape(input_features.shape)
    x = L0_attn_x
    mod = (_silu(L0_c) @ L0_wmod).reshape(L0_c.shape[0], 6, 1, -1)
    sa, ca, ga, sb, cb, gb = (mod[:, 0], mod[:, 1], mod[:, 2], mod[:, 3], mod[:, 4], mod[:, 5])
    ga = (2 * (ga >= 0) - 1) * jnp.maximum(jnp.abs(ga), 0.25)
    gb = (2 * (gb >= 0) - 1) * jnp.maximum(jnp.abs(gb), 0.25)
    h = _layernorm(x, axis=-1) * (1 + ca) + sa
    x = x + ga * _L0_attn_ref(h, L0_attn_Wi, L0_attn_conv_w, L0_attn_conv_b, L0_attn_Wg, L0_attn_bg, L0_attn_forget_base, L0_attn_Wo)
    h = _layernorm(x, axis=-1) * (1 + cb) + sb
    x = x + gb * _L0_ffn_ref(h, L0_ffn_centroids, L0_ffn_ln_g, L0_ffn_ln_b, L0_ffn_w1, L0_ffn_b1, L0_ffn_w2, L0_ffn_b2)
    return x

_drawn_inputs = setup_inputs


def setup_inputs(seed=0):
    import zlib

    import numpy as np

    out = dict(_drawn_inputs(seed))
    spreads = {'L0_attn_bg': (0.0, 0.8),
     'L0_ffn_ln_g': (1.0, 0.6),
     'L0_ffn_ln_b': (0.0, 0.8),
     'L0_ffn_b1': (0.0, 0.8),
     'L0_ffn_b2': (0.0, 0.402)}
    factors = {'L0_attn_conv_b': 5.366, 'L0_ffn_w1': 4.344, 'L0_ffn_w2': 3.413}
    for name, (base, spread) in spreads.items():
        noise = np.random.default_rng([zlib.crc32(name.encode()), seed]).standard_normal(out[name].shape)
        drawn = base * np.exp(spread * noise) if base else spread * noise
        out[name] = jnp.asarray(drawn.astype(out[name].dtype))
    for name, factor in factors.items():
        out[name] = (out[name] * factor).astype(out[name].dtype)
    return out
```

```python
from contextlib import ExitStack

import concourse.bass as bass
from concourse import mybir

ALU = mybir.AluOpType
ACT = mybir.ActivationFunctionType
AX = mybir.AxisListType
F32 = mybir.dt.float32
BF16 = mybir.dt.bfloat16
I32 = mybir.dt.int32
U32 = mybir.dt.uint32

P = 128
EPS = 1e-5

CONV_B, BG_F, BG_I, FORGET, CONV_W, LN_G, LN_B, COND, CENT, SMALL = 0, 3, 6, 9, 12, 24, 32, 40, 42, 50


def ge(eng, sem, value):
    if isinstance(value, int) and value <= 0:
        return
    eng.wait_ge(sem, value)


def ge_apart(eng, sem, value, passed):
    ge(eng, sem, value)
    if not isinstance(value, int):
        eng.sem_inc(passed, 1)


def adaln_block_kernel(nc, x_d, WiT_d, WgT_d, WoT_d, small_d, w1_d, b1_d, w2_d, b2_d, wmod_d, out_d):
    B, T, D = x_d.shape
    HID = WgT_d.shape[0]
    E, _, F = w1_d.shape
    TC = 512
    NC = T // TC
    NJ = TC // P
    NI = B * NJ
    NT = B * T // P
    HH = HID - P
    FJ = F // P
    G = 3
    NP = NT + E - 1
    RING = 4
    PAY = 2 * D + 4
    NM = 4 * G
    assert B == 2 and HH == 64 and D == P and T % TC == 0 and (NP - 3) % RING == 0

    ctx = ExitStack()
    with ctx:
        def sb(name, shape, dt=F32):
            return ctx.enter_context(nc.sbuf_tensor(name, shape, dt))

        def ps(name):
            return ctx.enter_context(nc.psum_tensor(name, [P, 512], F32))

        def sem(name):
            return ctx.enter_context(nc.semaphore(name))

        rows_d = nc.dram_tensor("rows_d", [B * T, PAY], F32, kind="Internal").ap()

        WiT = sb("WiT", [P, 2 * HID])
        WgA = sb("WgA", [P, 2 * HID])
        WgH = sb("WgH", [P, 2 * HID])
        WgD = sb("WgD", [P, 2, P])
        WoA = sb("WoA", [P, D])
        WoH = sb("WoH", [P, D])
        WoAg = sb("WoAg", [P, B, D])
        WoHg = sb("WoHg", [P, D])
        small = sb("small", [P, SMALL])
        wmod = sb("wmod", [P, 6 * D])
        w1 = sb("w1", [P, E * F])
        b2B = sb("b2B", [P, E * D])
        ident = sb("ident", [P, P])
        below = sb("below", [P, P], BF16)
        ones = sb("ones", [P, P], BF16)
        onesf = sb("onesf", [P, NT * E])
        iotaE = sb("iotaE", [P, E])
        iotaS = sb("iotaS", [P, P])
        iotaP = sb("iotaP", [P, NP])
        iotaT = sb("iotaT", [P, NT])
        part1 = sb("part1", [P, 1])
        epsc = sb("epsc", [P, 1])
        mhalf = sb("mhalf", [P, NI])

        silu = sb("silu", [P, B])
        siluB = sb("siluB", [P, B, P])
        modT = sb("modT", [P, 4])
        gaB = sb("gaB", [P, B, D])
        sbB = sb("sbB", [P, B, D])
        cbB = sb("cbB", [P, B, D])
        gbB = sb("gbB", [P, B, D])
        gbdiff = sb("gbdiff", [P, D])
        mtmp = sb("mtmp", [P, 2, B, D])
        decay = sb("decay", [P, 5, G])
        bgh = sb("bgh", [P, 2 * G])

        xs = sb("xs", [P, NC, NI, D])
        up = sb("up", [P, G, 3 + T])
        uc = sb("uc", [P, G, TC])
        gg = sb("gg", [P, G, T])
        n1 = sb("n1", [P, NI, D])
        hT = sb("hT", [P, B, TC])
        st = sb("st", [P, 3, NI, 6])
        mv = sb("mv", [P, 3, NI, 2])
        ve = sb("ve", [P, 3, NI])
        rs = sb("rs", [P, 3, NI])
        tf = sb("tf", [P, G, TC])
        ti = sb("ti", [P, G, TC])
        av = sb("av", [P, G, TC])
        bt = sb("bt", [P, G, TC])
        vx = sb("vx", [P, G, TC])
        hh = sb("hh", [P, G, TC])
        hc = sb("hc", [P, G])
        gh = sb("gh", [P, G, TC])
        h2 = sb("h2", [P, NI, D])
        h2T = sb("h2T", [P, NI, P])
        pay = sb("pay", [P, NI, PAY])
        am = sb("am", [P, NI])
        oh = sb("oh", [P, 2, NI, E])
        em = sb("em", [P, NI])
        O = sb("O", [P, B, NC * NJ, E], BF16)

        w2 = up[:, :, :].rearrange("p g t -> p (g t)")[:, 0:E * F]
        b1B = gg[:, :, :].rearrange("p g t -> p (g t)")[:, 0:E * F]

        tot = tf[:, 0, 0:NT * E]
        cum = tf[:, 1, 0:NT * E]
        posb = ti[:, 0, 0:NT * E]
        posO = ti[:, 1, 0:NT * E]
        s8 = sb("s8", [P, 8, E])
        s8i = sb("s8i", [P, 2, E], I32)
        pos = sb("pos", [P, 3, NT])
        posi = sb("posi", [P, 3, NT], I32)
        slotA = sb("slotA", [P, NT, P], BF16)
        pageF = sb("pageF", [P, NT, NP], BF16)
        pageR = sb("pageR", [P, NT, 2, NP], BF16)
        ends = vx[:, 0, 0:NP * E].rearrange("p (n e) -> p n e", e=E)
        val = sb("val", [P, 4, NP])
        gidx = sb("gidx", [P, NP], U32)
        sidx = sb("sidx", [P, NP], U32)
        isb1 = sb("isb1", [P, NP])
        eof = sb("eof", [P, NP])
        eoi = sb("eoi", [P, NP], I32)

        pg = pay[:, 0:RING, :]
        gix = sb("gix", [P, RING], U32)
        six = sb("six", [P, RING], U32)
        og = h2[:, 0:RING, :]
        gs = n1[:, 0:2, :]
        t1 = n1[:, 2:4, :]
        xT = n1[:, 4, :]
        ta = sb("ta", [P, 2])
        al = sb("al", [P, 2])
        hs = h2T[:, 0:FJ, :].rearrange("p j f -> p (j f)")
        hTs = h2T[:, FJ:2 * FJ, :].rearrange("p j f -> p (j f)")

        psT = [ps("psT0"), ps("psT1")]
        psM = [ps(f"psM{i}") for i in range(4)]
        psO = [ps("psO0"), ps("psO1")]
        psH, psHT, psY = psM[0], psM[1], [psM[2], psM[3]]

        s_small, s_wmod, s_wi, s_wg, s_wo = sem("small_in"), sem("wmod_in"), sem("wi_in"), sem("wg_in"), sem("wo_in")
        s_x = [sem(f"x{c}_in") for c in range(NC)]
        s_ew, s_out = sem("experts_in"), sem("out_written")
        s_id0, s_const, s_zero, s_iota = sem("ident_zeroed"), sem("ident"), sem("zeroed"), sem("iotas")
        s_cond, s_silu, s_siluB, s_mod, s_modev = sem("cond_tanh"), sem("silu"), sem("siluB"), sem("mod_mm"), sem("mod_copied")
        s_prep, s_dexp, s_decay, s_wog, s_wgd = sem("prep"), sem("decay_exp"), sem("decay"), sem("wo_gated"), sem("wg_diag")
        s_st = [sem(f"ln{n}_stats") for n in range(3)]
        s_mv = [sem(f"ln{n}_mean_var") for n in range(3)]
        s_ve = [sem(f"ln{n}_var_eps") for n in range(3)]
        s_rs = [sem(f"ln{n}_rstd") for n in range(3)]
        s_n1, s_xt, s_hT = sem("n1"), sem("x_turned"), sem("hT")
        s_mm, s_ev = sem("proj_mm"), sem("proj_read")
        s_conv, s_a, s_sq, s_y, s_beta = sem("conv"), sem("alpha"), sem("alpha_sq"), sem("one_less_sq"), sem("beta")
        s_v, s_xin, s_scan, s_carry, s_g = sem("gated_beta"), sem("rec_in"), sem("scan"), sem("carry"), sem("gelu_h")
        s_op, s_x1, s_n2, s_h2m, s_h2 = sem("wo_mm"), sem("x1"), sem("n2"), sem("h2_scaled"), sem("h2")
        s_rm, s_r, s_xn = sem("gb_h2"), sem("resid"), sem("xn")
        s_h2p, s_h2T, s_aff, s_am, s_ar = sem("h2_turned"), sem("h2T"), sem("aff_mm"), sem("aff_max"), sem("aff_read")
        s_rt, s_O, s_row = sem("route_steps"), sem("onehot"), sem("rows_written")
        s_cnt, s_tab, s_tabA, s_idx, s_tabs = sem("counts_mm"), sem("table_steps"), sem("slot_onehots"), sem("index_mm"), sem("tables")
        s_passed = [sem(f"{e}_passed") for e in ("dve", "pool", "sp")]
        s_gix, s_six = sem("gather_index"), sem("scatter_index")
        s_gat = [sem(f"gathered{q}") for q in range(RING)]
        s_sct = [sem(f"scattered{q}") for q in range(RING)]
        s_pt, s_pxT, s_p1, s_ph, s_pht, s_phT, s_p2 = (sem("page_turned"), sem("page_xT"), sem("page_mm1"),
            sem("page_h"), sem("page_h_turned"), sem("page_hT"), sem("page_mm2"))
        s_al, s_t1 = [sem(f"page_alpha{h}") for h in range(2)], [sem(f"page_y{h}") for h in range(2)]
        s_ta, s_gs, s_t2, s_o = sem("page_tanh"), sem("page_gate"), sem("page_yg"), sem("page_out")

        def tm(s):
            return bass.ds(s * TC, TC)

        def bc(ap, n):
            return ap.unsqueeze(1).to_broadcast([P, n, ap.shape[-1]])

        block = ctx.enter_context(nc.Block())

        @block.sync
        def _(sp):
            sp.dma_start(small[:, :], small_d).then_inc(s_small, 16)
            sp.dma_start(wmod[:, :], wmod_d).then_inc(s_wmod, 16)

            def load_x(c):
                for b in range(B):
                    sp.dma_start(xs[:, c, b * NJ:(b + 1) * NJ, :],
                                 x_d[b, c * TC:(c + 1) * TC, :].rearrange("(j p) d -> p j d", p=P)).then_inc(s_x[c], 16)

            load_x(0)
            sp.dma_start(WiT[:, :], WiT_d).then_inc(s_wi, 16)
            sp.dma_start(WgA[:, :], WgT_d[0:P, :]).then_inc(s_wg, 16)
            for b in range(B):
                sp.dma_start(WgH[b * HH:(b + 1) * HH, :], WgT_d[P:HID, :]).then_inc(s_wg, 16)
            sp.dma_start(WoA[:, :], WoT_d[0:P, :]).then_inc(s_wo, 16)
            for b in range(B):
                sp.dma_start(WoH[b * HH:(b + 1) * HH, :], WoT_d[P:HID, :]).then_inc(s_wo, 16)
            for c in range(1, NC):
                load_x(c)
            sp.dma_start(w1[:, :].rearrange("d (e f) -> d e f", e=E), w1_d.rearrange("e d f -> d e f")).then_inc(s_ew, 16)
            sp.dma_start(b2B[:, :], b2_d.partition_broadcast(P)).then_inc(s_ew, 16)

            def store_rows(c):
                ge_apart(sp, s_xn, NI * c + NI, s_passed[2])
                ge_apart(sp, s_r, 2 * c + 2, s_passed[2])
                ge_apart(sp, s_rt, 3 * c + 1, s_passed[2])
                for b in range(B):
                    sp.dma_start(rows_d[bass.ds(b * T + c * TC, TC), :].rearrange("(j p) d -> p j d", p=P),
                                 pay[:, b * NJ:(b + 1) * NJ, :]).then_inc(s_row, 16)

            store_rows(0)
            with sp.Fori(1, NC - 1) as c:
                store_rows(c)
            sp.wait_ge(s_conv, 12 * NC)
            sp.dma_start(w2.rearrange("p (n d) -> p n d", d=D),
                         w2_d.rearrange("e (j p) d -> p (e j) d", p=P)).then_inc(s_ew, 16)
            sp.wait_ge(s_g, NC)
            sp.dma_start(b1B, b1_d.partition_broadcast(P)).then_inc(s_ew, 16)
            store_rows(NC - 1)
            sp.wait_ge(s_row, 16 * B * NC)

        @block.tensor
        def _(pe):
            pe.wait_ge(s_wmod, 16)
            pe.wait_ge(s_silu, 2)
            for n in range(2):
                mm = pe.matmul(psT[0][:, 2 * n:2 * n + 2], wmod[:, n * D:(n + 1) * D], silu[:, :], start=True, stop=True)
            mm.then_inc(s_mod, 1)
            pe.wait_ge(s_siluB, B)
            for b in range(B):
                pe.matmul(psM[b][:, :], siluB[:, b, :], wmod[:, 2 * D:6 * D], start=True, stop=True).then_inc(s_mod, 1)

            def turn_x(c):
                for b in range(B):
                    ge(pe, s_n1, NI * c + NJ * (b + 1))
                    if isinstance(c, int) and c == 0:
                        pe.wait_ge(s_modev, 4)
                    for j in range(NJ):
                        mm = pe.transpose(psT[b][:, j * P:(j + 1) * P], n1[:, b * NJ + j, :], ident[:, :])
                    mm.then_inc(s_xt, 1)

            def project(c, k, parts):
                ge(pe, s_ev, NM * c + k - 3)
                for out, lhsT, rhs, start, stop in parts:
                    mm = pe.matmul(out, lhsT, rhs, start=start, stop=stop, skip_group_check=True)
                mm.then_inc(s_mm, 1)

            def project_in(c):
                ge(pe, s_hT, 2 * c + 2)
                for k in range(6):
                    ch = HID * (1 - k // 3)
                    ring = psM[k % 4]
                    g = k % 3
                    if g < 2:
                        project(c, k, [(ring[:, :], WiT[:, ch:ch + P], hT[:, g, :], True, True)])
                    else:
                        project(c, k, [(ring[b * HH:(b + 1) * HH, :], WiT[:, ch + P:ch + HID], hT[:, b, :], True, True)
                                       for b in range(B)])

            def project_gates(c):
                ge(pe, s_conv, 12 * c + 12)
                for k in range(6, 12):
                    o = HID * ((k - 6) // 3)
                    ring = psM[k % 4]
                    g = k % 3
                    if g < 2:
                        half = slice(g * HH, (g + 1) * HH)
                        project(c, k, [(ring[:, :], WgA[:, o:o + P], uc[:, g, :], True, False),
                                       (ring[:, :], WgH[half, o:o + P], uc[half, 2, :], False, True)])
                    else:
                        project(c, k, [(ring[:, :], WgD[:, (k - 6) // 3, :], uc[:, 2, :], True, False)]
                                + [(ring[b * HH:(b + 1) * HH, :], WgA[:, o + P:o + HID], uc[:, b, :], False, True)
                                   for b in range(B)])

            def project_out(c):
                ge(pe, s_g, c + 1)
                ge(pe, s_ar, c)
                for b in range(B):
                    half = slice(b * HH, (b + 1) * HH)
                    for j in range(NJ):
                        out = psO[b][:, j * D:(j + 1) * D]
                        pe.matmul(out, gh[:, b, j * P:(j + 1) * P], WoAg[:, b, :], start=True, stop=False)
                        mm = pe.matmul(out, gh[half, 2, j * P:(j + 1) * P], WoHg[half, :], start=False, stop=True)
                    mm.then_inc(s_op, 1)

            def affinities(c):
                for b in range(B):
                    ge(pe, s_h2, 2 * c + b + 1)
                    for j in range(NJ):
                        mm = pe.transpose(psT[b][:, j * P:(j + 1) * P], h2[:, b * NJ + j, :], ident[:, :])
                    mm.then_inc(s_h2p, 1)
                ge(pe, s_x1, 2 * c + 2)
                for b in range(B):
                    ge(pe, s_h2T, 2 * c + b + 1)
                    for j in range(NJ):
                        i = b * NJ + j
                        mm = pe.matmul(psO[0][:, i * E:(i + 1) * E], h2T[:, i, :], small[:, CENT:CENT + E],
                                       start=True, stop=True)
                mm.then_inc(s_aff, 1)

            pe.wait_ge(s_const, 1)
            pe.wait_ge(s_wi, 16)
            turn_x(0)
            project_in(0)
            pe.wait_ge(s_wg, 48)
            pe.wait_ge(s_wgd, 4)
            project_gates(0)
            pe.wait_ge(s_wog, 3)
            with pe.Fori(1, NC) as c:
                turn_x(c)
                project_in(c)
                project_out(c - 1)
                project_gates(c)
                affinities(c - 1)
            project_out(NC - 1)
            affinities(NC - 1)

            onehots = O[:, :, :, :].rearrange("p b t e -> p (b t e)")
            pe.wait_ge(s_O, 2 * NC)
            pe.matmul(psM[0][:, 0:NT * E], below[:, :], onehots, start=True, stop=True).then_inc(s_cnt, 1)
            pe.matmul(psM[1][:, 0:NT * E], ones[:, :], onehots, start=True, stop=True).then_inc(s_cnt, 1)
            for t in range(NT):
                if t % 8 == 0:
                    pe.wait_ge(s_tabA, t + 8)
                mm = pe.matmul(psM[2][:, 0:2 * NP], slotA[:, t, :], pageR[:, t, :, :].rearrange("p a n -> p (a n)"),
                               start=(t == 0), stop=(t == NT - 1))
            mm.then_inc(s_idx, 1)

            def expert(k):
                return pe.value_load(eoi[0:1, bass.ds(k, 1)], min_val=0, max_val=E - 1)

            def turn_page(k, q, lap):
                pe.wait_ge(s_gat[q], 16 * (lap + 1))
                ge(pe, s_pxT, k)
                pe.transpose(psT[0][:, 0:P], pg[:, q, 0:D], ident[:, :]).then_inc(s_pt, 1)

            def up_page(k, e):
                pe.wait_ge(s_pxT, k + 1)
                ge(pe, s_ph, k)
                pe.matmul(psH[:, :], xT, w1[:, bass.ds(e * F, F)], start=True, stop=True).then_inc(s_p1, 1)

            def turn_h(k):
                pe.wait_ge(s_ph, k + 1)
                ge(pe, s_phT, k)
                for j in range(FJ):
                    mm = pe.transpose(psHT[:, j * P:(j + 1) * P], hs[:, j * P:(j + 1) * P], ident[:, :])
                mm.then_inc(s_pht, 1)

            def down_page(k, q, lap, e):
                pe.wait_ge(s_phT, k + 1)
                ge(pe, s_t1[q % 2], 2 * lap + q // 2)
                for j in range(FJ):
                    mm = pe.matmul(psY[q % 2][:, 0:D], hTs[:, j * P:(j + 1) * P], w2[:, bass.ds(e * F + j * D, D)],
                                   start=(j == 0), stop=(j == FJ - 1))
                mm.then_inc(s_p2, 1)

            pe.wait_ge(s_tabs, 3)
            pe.wait_ge(s_ew, 64)
            turn_page(0, 0, 0)
            up_page(0, expert(0))
            turn_page(1, 1, 0)

            def page(k, q, lap, last=NP):
                turn_h(k)
                if not isinstance(k, int) or k + 1 < NP:
                    up_page(k + 1, expert(k + 1))
                if not isinstance(k, int) or k + 2 < NP:
                    turn_page(k + 2, (q + 2) % RING, lap + (q + 2) // RING)
                down_page(k, q, lap, expert(k))

            for k in range(RING):
                page(k, k, 0)
            with pe.Fori(1, NP // RING) as lap:
                for q in range(RING):
                    page(lap * RING + q, q, lap)
            for k in range(NP // RING * RING, NP):
                page(k, k % RING, k // RING)

        @block.scalar
        def _(act):
            act.wait_ge(s_small, 16)
            act.activation(silu[:, :], small[:, COND:COND + B], ACT.Tanh, scale=0.5).then_inc(s_cond, 1)
            act.wait_ge(s_prep, 3)
            act.activation(decay[:, 1, :], decay[:, 0, :], ACT.Exp).then_inc(s_dexp, 1)

            def scale_hT(c):
                for b in range(B):
                    ge(act, s_xt, 2 * c + b + 1)
                    ge(act, s_mm, NM * (c - 1) + 6)
                    act.activation(hT[:, b, :], psT[b][:, :], ACT.Identity, bias=modT[:, b:b + 1],
                                   scale=modT[:, 2 + b:3 + b]).then_inc(s_hT, 1)

            def read_in(c):
                for g in range(G):
                    ge(act, s_mm, NM * c + g + 1)
                    act.activation(up[:, g, bass.ds(c * TC + 3, TC)], psM[g][:, :], ACT.Copy).then_inc(s_ev, 1)
                for g in range(G):
                    ge(act, s_mm, NM * c + 3 + g + 1)
                    act.activation(gg[:, g, tm(c)], psM[(3 + g) % 4][:, :], ACT.Gelu).then_inc(s_ev, 1)

            def read_gates(c):
                for k in range(6, 12):
                    g = k % 3
                    ge(act, s_mm, NM * c + k + 1)
                    if k == 9:
                        ge(act, s_v, c)
                    act.activation((tf if k < 9 else ti)[:, g, :], psM[k % 4][:, :], ACT.Tanh,
                                   bias=bgh[:, k - 6:k - 5], scale=0.5).then_inc(s_ev, 1)

            def alpha_beta(c):
                ge(act, s_scan, 3 * c)
                for g in range(G):
                    ge(act, s_ev, NM * c + 7 + g)
                    act.activation(av[:, g, :], tf[:, g, :], ACT.Exp, bias=decay[:, 4, g:g + 1],
                                   scale=decay[:, 4, g:g + 1]).then_inc(s_a, 1)
                ge(act, s_a, 3 * c + 3)
                act.activation(tf[:, :, :], av[:, :, :], ACT.Square).then_inc(s_sq, 1)
                ge(act, s_y, c + 1)
                act.activation(bt[:, :, :], bt[:, :, :], ACT.Sqrt, bias=epsc[:, :]).then_inc(s_beta, 1)

            def copy_h2T(c):
                for b in range(B):
                    ge(act, s_h2p, 2 * c + b + 1)
                    ge(act, s_aff, c)
                    act.activation(h2T[:, b * NJ:(b + 1) * NJ, :].rearrange("p j t -> p (j t)"), psT[b][:, :],
                                   ACT.Copy).then_inc(s_h2T, 1)

            act.wait_ge(s_modev, 2)
            scale_hT(0)
            act.wait_ge(s_zero, 1)
            read_in(0)
            act.wait_ge(s_prep, 5)
            read_gates(0)
            act.wait_ge(s_decay, 8)
            act.wait_ge(s_iota, 1)
            alpha_beta(0)
            with act.Fori(1, NC) as c:
                scale_hT(c)
                read_in(c)
                read_gates(c)
                copy_h2T(c - 1)
                alpha_beta(c)
            copy_h2T(NC - 1)

            def expert(k):
                return act.value_load(eoi[0:1, bass.ds(k, 1)], min_val=0, max_val=E - 1)

            def scale_page(k):
                e = expert(k)
                act.wait_ge(s_pt, k + 1)
                ge(act, s_p1, k)
                act.activation(xT, psT[0][:, 0:P], ACT.Identity, bias=small[:, bass.ds(LN_B + e, 1)],
                               scale=small[:, bass.ds(LN_G + e, 1)]).then_inc(s_pxT, 1)

            def page(k, q, lap):
                act.wait_ge(s_pht, k + 1)
                ge(act, s_p2, k)
                act.activation(hTs, psHT[:, :], ACT.Relu).then_inc(s_phT, 1)
                if not isinstance(k, int) or k + 2 < NP:
                    scale_page(k + 2)
                act.wait_ge(s_gat[q], 16 * (lap + 1))
                ge(act, s_al[q % 2], 2 * lap + q // 2)
                act.activation(ta[:, q % 2:q % 2 + 1], pg[:, q, 2 * D:2 * D + 1], ACT.Tanh, scale=0.5).then_inc(s_ta, 1)

            act.wait_ge(s_tabs, 3)
            scale_page(0)
            scale_page(1)
            for k in range(RING):
                page(k, k, 0)
            with act.Fori(1, NP // RING) as lap:
                for q in range(RING):
                    page(lap * RING + q, q, lap)
            for k in range(NP // RING * RING, NP):
                page(k, k % RING, k // RING)

        @block.vector
        def _(dve):
            v = dve
            steps = [0]

            def prep(ins):
                ins.then_inc(s_prep, 1)
                steps[0] += 1
                v.wait_ge(s_prep, steps[0])

            v.wait_ge(s_small, 16)
            prep(v.tensor_scalar(decay[:, 0, :], small[:, FORGET:FORGET + G], -1.0, None, ALU.mult))
            prep(v.tensor_tensor(decay[:, 3, :], small[:, FORGET:FORGET + G], decay[:, 0, :], ALU.max))
            prep(v.tensor_scalar(decay[:, 0, :], decay[:, 3, :], -1.0, None, ALU.mult))
            prep(v.tensor_scalar(bgh[:, :], small[:, BG_F:BG_F + 2 * G], 0.5, None, ALU.mult))
            prep(v.tensor_scalar(decay[:, 3, :], small[:, FORGET:FORGET + G], 0.0, -4.0, ALU.max, ALU.mult))
            v.wait_ge(s_cond, 1)
            v.scalar_tensor_tensor(out=silu[:, :], in0=silu[:, :], scalar=1.0, in1=small[:, COND:COND + B],
                                   op0=ALU.add, op1=ALU.mult).then_inc(s_silu, 1)
            v.wait_ge(s_silu, 1)
            v.tensor_scalar(silu[:, :], silu[:, :], 0.5, None, ALU.mult).then_inc(s_silu, 1)
            v.wait_ge(s_silu, 2)
            v.wait_ge(s_iota, 1)
            for b in range(B):
                v.tensor_scalar(siluB[:, b, :], iotaS[:, :], 0.0, silu[:, b:b + 1], ALU.mult,
                                ALU.add).then_inc(s_siluB, 1)
            v.wait_ge(s_mod, 1)
            v.tensor_copy(modT[:, 0:2], psT[0][:, 0:2]).then_inc(s_modev, 1)
            v.tensor_scalar(modT[:, 2:4], psT[0][:, 2:4], 1.0, None, ALU.add).then_inc(s_modev, 1)

            def ln_stats(n, c, tile):
                for i in range(NI):
                    v.bn_stats(st[:, n, i, :], tile(i)).then_inc(s_st[n], 1)
                ge_apart(v, s_st[n], NI * c + NI, s_passed[0])
                for i in range(NI):
                    v.bn_aggr(mv[:, n, i, :], st[:, n, i, :]).then_inc(s_mv[n], 1)

            def ln_out(n, c, tile, out, done):
                ge(v, s_rs[n], c + 1)
                for i in range(NI):
                    v.tensor_scalar(out(i), tile(i), mv[:, n, i, 0:1], rs[:, n, i:i + 1], ALU.subtract,
                                    ALU.mult).then_inc(done, 1)

            def ln1(c):
                ln_stats(0, c, lambda i: xs[:, c, i, :])
                ge(v, s_xt, 2 * c)
                ln_out(0, c, lambda i: xs[:, c, i, :], lambda i: n1[:, i, :], s_n1)

            def conv(c):
                ge(v, s_ev, NM * c + 3)
                for g in range(G):
                    v.tensor_scalar(uc[:, g, :], up[:, g, bass.ds(c * TC + 3, TC)],
                                    small[:, CONV_W + 9 + g:CONV_W + 10 + g], small[:, CONV_B + g:CONV_B + g + 1],
                                    ALU.mult, ALU.add).then_inc(s_conv, 1)
                for n in range(1, 4):
                    for g in range(G):
                        ge(v, s_conv, 12 * c + 3 * n + g - 2)
                        w = CONV_W + 3 * (3 - n) + g
                        v.scalar_tensor_tensor(out=uc[:, g, :], in0=up[:, g, bass.ds(c * TC + 3 - n, TC)],
                                               scalar=small[:, w:w + 1], in1=uc[:, g, :], op0=ALU.mult,
                                               op1=ALU.add).then_inc(s_conv, 1)

            def residual(c):
                for b in range(B):
                    ge(v, s_op, 2 * c + b + 1)
                    xb = xs[:, c, b * NJ:(b + 1) * NJ, :].rearrange("p j d -> p (j d)")
                    v.tensor_tensor(xb, xb, psO[b][:, :], ALU.add).then_inc(s_x1, 1)
                ge_apart(v, s_x1, 2 * c + 2, s_passed[0])
                ln_stats(1, c, lambda i: xs[:, c, i, :])
                ge(v, s_h2p, 2 * c)
                ge(v, s_rm, 2 * c)
                ln_out(1, c, lambda i: xs[:, c, i, :], lambda i: h2[:, i, :], s_n2)
                for b in range(B):
                    ge(v, s_h2m, 2 * c + b + 1)
                    hb = h2[:, b * NJ:(b + 1) * NJ, :]
                    v.tensor_tensor(hb, hb, bc(sbB[:, b, :], NJ), ALU.add).then_inc(s_h2, 1)
                ge(v, s_h2, 2 * c + 2)
                ln_stats(2, c, lambda i: h2[:, i, :])
                ge(v, s_row, 16 * B * c)
                ln_out(2, c, lambda i: h2[:, i, :], lambda i: pay[:, i, 0:D], s_xn)
                for b in range(B):
                    ge(v, s_rm, 2 * c + b + 1)
                    rb = pay[:, b * NJ:(b + 1) * NJ, D:2 * D]
                    v.tensor_tensor(rb, rb, xs[:, c, b * NJ:(b + 1) * NJ, :], ALU.add).then_inc(s_r, 1)

            def recur(c):
                ge(v, s_beta, c + 1)
                v.scalar_tensor_tensor(out=vx[:, :, :], in0=ti[:, :, :], scalar=1.0, in1=bt[:, :, :],
                                       op0=ALU.add, op1=ALU.mult).then_inc(s_v, 1)
                ge(v, s_xin, c + 1)
                ge(v, s_g, c)
                for g in range(G):
                    if isinstance(c, int) and c == 0:
                        first = 0.0
                    else:
                        first = hc[:, g:g + 1]
                        if g == 0:
                            ge(v, s_carry, c)
                    v.tensor_tensor_scan(hh[:, g, :], av[:, g, :], vx[:, g, :], first, ALU.mult,
                                         ALU.add).then_inc(s_scan, 1)
                ge(v, s_scan, 3 * c + 3)
                v.tensor_copy(hc[:, :], hh[:, :, TC - 1]).then_inc(s_carry, 1)

            def route(c):
                ge(v, s_aff, c + 1)
                aff = psO[0][:, 0:NI * E].rearrange("p (i e) -> p i e", e=E)
                v.tensor_reduce(am[:, :], aff, AX.X, ALU.max).then_inc(s_am, 1)
                ge(v, s_am, c + 1)
                v.tensor_copy(pay[:, :, 2 * D], am[:, :]).then_inc(s_rt, 1)
                v.tensor_tensor(oh[:, 0, :, :], aff, am[:, :].unsqueeze(2).to_broadcast([P, NI, E]),
                                ALU.is_equal).then_inc(s_ar, 1)
                ge(v, s_ar, c + 1)
                v.tensor_tensor(oh[:, 1, :, :], oh[:, 0, :, :], bc(iotaE[:, :], NI), ALU.mult).then_inc(s_rt, 1)
                ge(v, s_rt, 3 * c + 2)
                v.tensor_reduce(em[:, :], oh[:, 1, :, :], AX.X, ALU.min).then_inc(s_rt, 1)
                ge(v, s_rt, 3 * c + 3)
                for b in range(B):
                    v.tensor_tensor(O[:, b, bass.ds(c * NJ, NJ), :], bc(iotaE[:, :], NJ),
                                    em[:, b * NJ:(b + 1) * NJ].unsqueeze(2).to_broadcast([P, NJ, E]),
                                    ALU.is_equal).then_inc(s_O, 1)

            v.wait_ge(s_x[0], 32)
            ln1(0)

            v.wait_ge(s_wg, 48)
            v.wait_ge(s_zero, 1)
            for n in range(2):
                o = HID * n + P
                for b in range(B):
                    half = slice(b * HH, (b + 1) * HH)
                    v.tensor_copy(WgD[half, n, half], WgH[half, o:o + HH]).then_inc(s_wgd, 1)

            for b in range(B):
                v.wait_ge(s_mod, 2 + b)
                prep(v.tensor_copy(gaB[:, b, :], psM[b][:, 0:D]))
                prep(v.tensor_copy(sbB[:, b, :], psM[b][:, D:2 * D]))
                prep(v.tensor_scalar(cbB[:, b, :], psM[b][:, 2 * D:3 * D], 1.0, None, ALU.add))
                v.tensor_copy(gbB[:, b, :], psM[b][:, 3 * D:4 * D]).then_inc(s_modev, 1)
            conv(0)
            v.wait_ge(s_modev, 2 + B)
            for gate in (gaB, gbB):
                prep(v.tensor_scalar(mtmp[:, 0, :, :], gate[:, :, :], -1.0, None, ALU.mult))
                prep(v.tensor_tensor(mtmp[:, 0, :, :], mtmp[:, 0, :, :], gate[:, :, :], ALU.max))
                prep(v.tensor_scalar(mtmp[:, 0, :, :], mtmp[:, 0, :, :], 0.25, None, ALU.max))
                prep(v.tensor_scalar(mtmp[:, 1, :, :], gate[:, :, :], 0.0, 2.0, ALU.is_ge, ALU.mult))
                prep(v.scalar_tensor_tensor(out=gate[:, :, :], in0=mtmp[:, 1, :, :], scalar=-1.0,
                                            in1=mtmp[:, 0, :, :], op0=ALU.add, op1=ALU.mult))
            prep(v.tensor_tensor(gbdiff[:, :], gbB[:, 1, :], gbB[:, 0, :], ALU.subtract))
            v.wait_ge(s_wo, 48)
            v.scalar_tensor_tensor(out=WoAg[:, :, :], in0=gaB[:, :, :], scalar=0.5, in1=bc(WoA[:, :], B),
                                   op0=ALU.mult, op1=ALU.mult).then_inc(s_wog, 1)
            for b in range(B):
                half = slice(b * HH, (b + 1) * HH)
                v.scalar_tensor_tensor(out=WoHg[half, :], in0=WoH[half, :], scalar=0.5, in1=gaB[half, b, :],
                                       op0=ALU.mult, op1=ALU.mult).then_inc(s_wog, 1)
            v.wait_ge(s_dexp, 1)
            z, s, s2, acc = decay[:, 1, :], decay[:, 0, :], decay[:, 2, :], decay[:, 4, :]
            prep(v.tensor_scalar(s2, z, 2.0, None, ALU.add))
            prep(v.reciprocal(s2, s2))
            prep(v.tensor_tensor(s, z, s2, ALU.mult))
            prep(v.tensor_tensor(s2, s, s, ALU.mult))
            prep(v.tensor_scalar(acc, s2, 1.0 / 17, 1.0 / 15, ALU.mult, ALU.add))
            done = 0
            for n in (13, 11, 9, 7, 5, 3, 1):
                v.tensor_tensor(acc, acc, s2, ALU.mult).then_inc(s_decay, 1)
                done += 1
                v.wait_ge(s_decay, done)
                prep(v.tensor_scalar(acc, acc, 1.0 / n, None, ALU.add))
            prep(v.tensor_tensor(acc, acc, s, ALU.mult))
            v.scalar_tensor_tensor(out=acc, in0=acc, scalar=-8.0, in1=decay[:, 3, :], op0=ALU.mult,
                                   op1=ALU.add).then_inc(s_decay, 1)

            recur(0)
            for c in range(1, NC):
                v.wait_ge(s_x[c], 32)
            with v.Fori(1, NC) as c:
                ln1(c)
                conv(c)
                residual(c - 1)
                recur(c)
                route(c - 1)
            residual(NC - 1)
            route(NC - 1)

            tb = [0]

            def tab(ins):
                ins.then_inc(s_tab, 1)
                tb[0] += 1
                v.wait_ge(s_tab, tb[0])

            def et(ap):
                return ap.rearrange("p (e t) -> p e t", e=E)

            def te(ap):
                return ap.rearrange("p (t e) -> p e t", e=E)

            v.wait_ge(s_cnt, 2)
            v.wait_ge(s_iota, 2)
            tab(v.tensor_copy(et(tot), te(psM[1][:, 0:NT * E])))
            tab(v.tensor_tensor_scan(cum, onesf[:, :], tot, 0.0, ALU.mult, ALU.add))
            end = cum.rearrange("p (e t) -> p e t", e=E)[:, :, NT - 1]
            count, pages, pend, shift, low = (s8[:, n, :] for n in range(5))
            v.tensor_copy(low[:, 1:E], end[:, 0:E - 1]).then_inc(s_tab, 1)
            tab(v.memset(low[:, 0:1], 0.0))
            tb[0] += 1
            v.wait_ge(s_tab, tb[0])
            tab(v.tensor_tensor(count, end, low, ALU.subtract))
            tab(v.tensor_scalar(s8i[:, 0, :], count, float(P - 1), None, ALU.add))
            tab(v.tensor_scalar(s8i[:, 1, :], s8i[:, 0, :], 7, None, ALU.logical_shift_right))
            tab(v.tensor_copy(pages, s8i[:, 1, :]))
            tab(v.tensor_tensor_scan(pend, onesf[:, 0:E], pages, 0.0, ALU.mult, ALU.add))
            tab(v.tensor_tensor(shift, pend, pages, ALU.subtract))
            tab(v.scalar_tensor_tensor(out=shift, in0=shift, scalar=float(P), in1=low, op0=ALU.mult, op1=ALU.subtract))
            tab(v.tensor_tensor(posb, cum, tot, ALU.subtract))
            tab(v.tensor_tensor(et(posb), et(posb), shift.unsqueeze(2).to_broadcast([P, E, NT]), ALU.add))
            tab(v.tensor_tensor(et(posb), et(posb), te(psM[0][:, 0:NT * E]), ALU.add))
            tab(v.tensor_tensor(et(posO), et(posb), te(O[:, :, :, :].rearrange("p b t e -> p (b t e)")), ALU.mult))
            tab(v.tensor_reduce(pos[:, 0, :], posO.rearrange("p (e t) -> p t e", e=E), AX.X, ALU.add))
            tab(v.tensor_copy(posi[:, 0, :], pos[:, 0, :]))
            tab(v.tensor_scalar(posi[:, 1, :], posi[:, 0, :], 7, None, ALU.logical_shift_right))
            tab(v.tensor_scalar(posi[:, 2, :], posi[:, 0, :], P - 1, None, ALU.bitwise_and))
            tab(v.tensor_copy(pos[:, 1:3, :], posi[:, 1:3, :]))
            tab(v.tensor_tensor(pageF[:, :, :], bc(iotaP[:, :], NT),
                                pos[:, 1, :].unsqueeze(2).to_broadcast([P, NT, NP]), ALU.is_equal))
            tab(v.tensor_scalar(pageR[:, :, 0, :], pageF[:, :, :], part1[:, :], None, ALU.mult))
            tab(v.tensor_tensor(pageR[:, :, 1, :], pageF[:, :, :],
                                iotaT[:, :].unsqueeze(2).to_broadcast([P, NT, NP]), ALU.mult))
            for t in range(NT):
                v.tensor_scalar(slotA[:, t, :], iotaS[:, :], pos[:, 2, t:t + 1], None, ALU.is_equal).then_inc(s_tabA, 1)
            tab(v.tensor_tensor(ends, iotaP[:, :].unsqueeze(2).to_broadcast([P, NP, E]),
                                pend.unsqueeze(1).to_broadcast([P, NP, E]), ALU.is_ge))
            tab(v.tensor_reduce(eof[:, :], ends, AX.X, ALU.add))
            tab(v.tensor_scalar(eof[:, :], eof[:, :], float(E - 1), None, ALU.min))
            v.tensor_copy(eoi[:, :], eof[:, :]).then_inc(s_tabs, 1)
            v.wait_ge(s_idx, 1)
            tab(v.tensor_copy(val[:, 0, :], psM[2][:, 0:NP]))
            tab(v.scalar_tensor_tensor(out=val[:, 1, :], in0=psM[2][:, NP:2 * NP], scalar=float(P), in1=val[:, 0, :],
                                       op0=ALU.mult, op1=ALU.add))
            tab(v.tensor_scalar(val[:, 2, :], val[:, 1, :], -1.0, 0.0, ALU.add, ALU.max))
            v.tensor_copy(gidx[:, :], val[:, 2, :]).then_inc(s_tabs, 1)
            tab(v.tensor_scalar(val[:, 3, :], val[:, 1, :], 0.0, float(2 * B * T), ALU.is_equal, ALU.mult))
            tab(v.tensor_tensor(val[:, 3, :], val[:, 3, :], val[:, 2, :], ALU.add))
            tab(v.tensor_scalar(isb1[:, :], val[:, 2, :], float(T), None, ALU.is_ge))
            v.tensor_copy(sidx[:, :], val[:, 3, :]).then_inc(s_tabs, 1)

            def expert(k):
                return v.value_load(eoi[0:1, bass.ds(k, 1)], min_val=0, max_val=E - 1)

            def bias_h(k):
                e = expert(k)
                v.wait_ge(s_p1, k + 1)
                ge(v, s_pht, k)
                v.tensor_tensor(hs, psH[:, :], b1B[:, bass.ds(e * F, F)], ALU.add).then_inc(s_ph, 1)

            def page(k, q, lap):
                if not isinstance(k, int) or k + 1 < NP:
                    bias_h(k + 1)
                two = q % 2
                v.tensor_scalar(gs[:, two, :], gbdiff[:, :], isb1[:, bass.ds(k, 1)], None, ALU.mult).then_inc(s_gs, 1)
                v.wait_ge(s_ta, k + 1)
                v.tensor_scalar(al[:, two:two + 1], ta[:, two:two + 1], 1.0, 0.5, ALU.add, ALU.mult).then_inc(s_al[two], 1)
                v.wait_ge(s_gs, 2 * k + 1)
                v.tensor_tensor(gs[:, two, :], gs[:, two, :], gbB[:, 0, :], ALU.add).then_inc(s_gs, 1)
                e = expert(k)
                v.wait_ge(s_p2, k + 1)
                v.tensor_tensor(t1[:, two, :], psY[two][:, 0:D], b2B[:, bass.ds(e * D, D)], ALU.add).then_inc(s_t1[two], 1)
                v.wait_ge(s_t1[two], 2 * lap + q // 2 + 1)
                v.wait_ge(s_gs, 2 * k + 2)
                v.wait_ge(s_al[two], 2 * lap + q // 2 + 1)
                v.scalar_tensor_tensor(out=t1[:, two, :], in0=t1[:, two, :], scalar=al[:, two:two + 1],
                                       in1=gs[:, two, :], op0=ALU.mult, op1=ALU.mult).then_inc(s_t2, 1)
                v.wait_ge(s_t2, k + 1)
                ge(v, s_sct[q], 16 * lap)
                v.wait_ge(s_gat[q], 16 * (lap + 1))
                v.tensor_tensor(og[:, q, :], t1[:, two, :], pg[:, q, D:2 * D], ALU.add).then_inc(s_o, 1)

            v.wait_ge(s_tabs, 3)
            v.wait_ge(s_ew, 64)
            bias_h(0)
            for k in range(RING):
                page(k, k, 0)
            with v.Fori(1, NP // RING) as lap:
                for q in range(RING):
                    page(lap * RING + q, q, lap)
            for k in range(NP // RING * RING, NP):
                page(k, k % RING, k // RING)

        @block.gpsimd
        def _(pool):
            g = pool
            g.memset(ident[:, :], 0.0).then_inc(s_id0, 1)
            g.memset(below[:, :], 1.0)
            g.memset(up[:, :, 0:3], 0.0)
            g.memset(WgD[:, :, :], 0.0).then_inc(s_zero, 1)
            g.memset(ones[:, :], 1.0)
            g.iota(iotaS[:, :], pattern=[[1, P]], base=0, channel_multiplier=0, allow_small_or_imprecise_dtypes=True)
            g.memset(epsc[:, :], 1e-6)
            g.memset(mhalf[:, :], -0.5).then_inc(s_iota, 1)
            g.wait_ge(s_id0, 1)
            g.affine_select(out=ident[:, :], in_=ident[:, :], compare_op=ALU.not_equal, fill=1.0, base=0,
                            pattern=[[-1, P]], channel_multiplier=1).then_inc(s_const, 1)

            def rstd(n, c):
                ge_apart(g, s_mv[n], NI * c + NI, s_passed[1])
                g.tensor_scalar(ve[:, n, :], mv[:, n, :, 1], EPS, None, ALU.add).then_inc(s_ve[n], 1)
                ge(g, s_ve[n], c + 1)
                g.tensor_tensor(rs[:, n, :], ve[:, n, :], mhalf[:, :], ALU.pow).then_inc(s_rs[n], 1)

            def modulate(c):
                rstd(1, c)
                for b in range(B):
                    ge(g, s_n2, NI * c + NJ * (b + 1))
                    hb = h2[:, b * NJ:(b + 1) * NJ, :]
                    g.tensor_tensor(hb, hb, bc(cbB[:, b, :], NJ), ALU.mult).then_inc(s_h2m, 1)
                ge(g, s_row, 16 * B * c)
                rstd(2, c)
                for b in range(B):
                    ge(g, s_h2, 2 * c + b + 1)
                    g.tensor_tensor(pay[:, b * NJ:(b + 1) * NJ, D:2 * D], h2[:, b * NJ:(b + 1) * NJ, :],
                                    bc(gbB[:, b, :], NJ), ALU.mult).then_inc(s_rm, 1)

            def recur(c):
                ge(g, s_sq, c + 1)
                ge_apart(g, s_v, c, s_passed[1])
                g.tensor_scalar(bt[:, :, :], tf[:, :, :], -1.0, 1.0, ALU.mult, ALU.add).then_inc(s_y, 1)
                ge(g, s_v, c + 1)
                g.tensor_tensor(vx[:, :, :], vx[:, :, :], uc[:, :, :], ALU.mult).then_inc(s_xin, 1)
                ge(g, s_scan, 3 * c + 3)
                ge(g, s_op, 2 * c)
                g.tensor_tensor(gh[:, :, :], gg[:, :, tm(c)], hh[:, :, :], ALU.mult).then_inc(s_g, 1)

            rstd(0, 0)
            g.wait_ge(s_zero, 1)
            g.affine_select(out=below[:, :], in_=below[:, :], compare_op=ALU.is_gt, fill=0.0, base=0,
                            pattern=[[1, P]], channel_multiplier=-1)
            g.memset(pay[:, :, 2 * D + 1:PAY], 0.0)
            g.iota(iotaE[:, :], pattern=[[1, E]], base=-E, channel_multiplier=0, allow_small_or_imprecise_dtypes=True)
            g.iota(iotaP[:, :], pattern=[[1, NP]], base=0, channel_multiplier=0, allow_small_or_imprecise_dtypes=True)
            g.iota(iotaT[:, :], pattern=[[1, NT]], base=0, channel_multiplier=0, allow_small_or_imprecise_dtypes=True)
            g.iota(part1[:, :], pattern=[[0, 1]], base=1, channel_multiplier=1, allow_small_or_imprecise_dtypes=True)
            g.memset(onesf[:, :], 1.0).then_inc(s_iota, 1)
            recur(0)
            with g.Fori(1, NC) as c:
                rstd(0, c)
                modulate(c - 1)
                recur(c)
            modulate(NC - 1)

            def gather(k, q):
                g.tensor_copy(gix[:, q:q + 1], gidx[:, bass.ds(k, 1)]).then_inc(s_gix, 1)
                ge_apart(g, s_gix, k + 1, s_passed[1])
                g.indirect_dma_start(out=pg[:, q, :], out_offset=None, in_=rows_d,
                                     in_offset=bass.IndirectOffsetOnAxis(ap=gix[:, q:q + 1], axis=0)).then_inc(s_gat[q], 16)

            def scatter(k, q):
                g.tensor_copy(six[:, q:q + 1], sidx[:, bass.ds(k, 1)]).then_inc(s_six, 1)
                g.wait_ge(s_six, k + 1)
                ge_apart(g, s_o, k + 1, s_passed[1])
                g.indirect_dma_start(out=out_d, out_offset=bass.IndirectOffsetOnAxis(ap=six[:, q:q + 1], axis=0),
                                     in_=og[:, q, :], in_offset=None, bounds_check=B * T - 1,
                                     oob_is_err=False).then_inc(s_sct[q], 16)

            g.wait_ge(s_tabs, 3)
            g.wait_ge(s_row, 16 * B * NC)
            for k in range(RING):
                gather(k, k)
            with g.Fori(0, NP // RING - 1) as lap:
                for q in range(RING):
                    scatter(lap * RING + q, q)
                    gather(lap * RING + RING + q, q)
            for k in range(NP // RING * RING - RING, NP):
                scatter(k, k % RING)
                if k + RING < NP:
                    gather(k + RING, k % RING)
            for q in range(RING):
                g.wait_ge(s_sct[q], 16 * len(range(q, NP, RING)))


def kernel(**inputs):
    import numpy as _np
    import concourse.bacc as _bacc
    from concourse.bass_utils import run_bass_kernel_spmd as _run

    a = {n: _np.asarray(v) for n, v in inputs.items()}

    def groups(v):
        return _np.stack([v[:P], v[:P], _np.concatenate([v[P:], v[P:]])], axis=1)

    H = a["L0_attn_Wg"].shape[1]
    bg = a["L0_attn_bg"]
    cw = a["L0_attn_conv_w"][:, 0, :]
    small = _np.concatenate(
        [groups(a["L0_attn_conv_b"]), groups(bg[:H]), groups(bg[H:]), groups(a["L0_attn_forget_base"])]
        + [groups(cw[:, k]) for k in range(cw.shape[1])]
        + [a["L0_ffn_ln_g"].T, a["L0_ffn_ln_b"].T, a["L0_c"].T, a["L0_ffn_centroids"].T], axis=1)
    arrays = {
        "x": a["L0_attn_x"], "WiT": a["L0_attn_Wi"].T, "WgT": a["L0_attn_Wg"].T, "WoT": a["L0_attn_Wo"].T,
        "small": small, "w1": a["L0_ffn_w1"], "b1": a["L0_ffn_b1"].reshape(-1), "w2": a["L0_ffn_w2"],
        "b2": a["L0_ffn_b2"].reshape(-1), "wmod": a["L0_wmod"],
    }
    nc = _bacc.Bacc("TRN2", target_bir_lowering=False, num_devices=1)
    arrays = {f"in_{n}": _np.ascontiguousarray(v) for n, v in arrays.items()}
    args = [nc.dram_tensor(n, v.shape, mybir.dt.from_np(v.dtype), kind="ExternalInput").ap() for n, v in arrays.items()]
    shape = a["L0_attn_x"].shape
    out = nc.dram_tensor("out", (shape[0] * shape[1], shape[2]), F32, kind="ExternalOutput").ap()
    adaln_block_kernel(nc, *args, out)
    r = _run(nc, [arrays], core_ids=[0])
    return r.results[0]["out"].reshape(shape)
```

```python
from contextlib import ExitStack

import concourse.bass as bass
from concourse import mybir

ALU = mybir.AluOpType
ACT = mybir.ActivationFunctionType
AX = mybir.AxisListType
F32 = mybir.dt.float32
BF16 = mybir.dt.bfloat16
I32 = mybir.dt.int32
U32 = mybir.dt.uint32

P = 128
EPS = 1e-5

CONV_B, BG_F, BG_I, FORGET, CONV_W, LN_G, LN_B, COND, CENT, SMALL = 0, 3, 6, 9, 12, 24, 32, 40, 42, 50


def ge(eng, sem, value):
    if isinstance(value, int) and value <= 0:
        return
    eng.wait_ge(sem, value)


def ge_apart(eng, sem, value, passed):
    ge(eng, sem, value)
    if not isinstance(value, int):
        eng.sem_inc(passed, 1)


def adaln_block_kernel(nc, x_d, WiT_d, WgT_d, WoT_d, small_d, w1_d, b1_d, w2_d, b2_d, wmod_d, out_d):
    B, T, D = x_d.shape
    HID = WgT_d.shape[0]
    E, _, F = w1_d.shape
    TC = 512
    NC = T // TC
    NJ = TC // P
    NI = B * NJ
    NT = B * T // P
    HH = HID - P
    FJ = F // P
    G = 3
    NP = NT + E - 1
    RING = 6
    HALF = RING // 2
    PAY = 2 * D + 4
    NM = 4 * G
    assert B == 2 and HH == 64 and D == P and T % TC == 0 and (NP - 3) % RING == 0

    ctx = ExitStack()
    with ctx:
        def sb(name, shape, dt=F32):
            return ctx.enter_context(nc.sbuf_tensor(name, shape, dt))

        def ps(name):
            return ctx.enter_context(nc.psum_tensor(name, [P, 512], F32))

        def sem(name):
            return ctx.enter_context(nc.semaphore(name))

        rows_d = nc.dram_tensor("rows_d", [B * T, PAY], F32, kind="Internal").ap()

        WiT = sb("WiT", [P, 2 * HID])
        WgA = sb("WgA", [P, 2 * HID])
        WgH = sb("WgH", [P, 2 * HID])
        WgD = sb("WgD", [P, 2, P])
        WoA = sb("WoA", [P, D])
        WoH = sb("WoH", [P, D])
        WoAg = sb("WoAg", [P, B, D])
        WoHg = sb("WoHg", [P, D])
        small = sb("small", [P, SMALL])
        wmod = sb("wmod", [P, 6 * D])
        w1 = sb("w1", [P, E * F])
        b2B = sb("b2B", [P, E * D])
        ident = sb("ident", [P, P])
        below = sb("below", [P, P], BF16)
        ones = sb("ones", [P, P], BF16)
        onesf = sb("onesf", [P, NT * E])
        iotaE = sb("iotaE", [P, E])
        iotaS = sb("iotaS", [P, P])
        iotaP = sb("iotaP", [P, NP])
        iotaT = sb("iotaT", [P, NT])
        part1 = sb("part1", [P, 1])
        epsc = sb("epsc", [P, 1])
        mhalf = sb("mhalf", [P, NI])

        silu = sb("silu", [P, B])
        siluB = sb("siluB", [P, B, P])
        modT = sb("modT", [P, 4])
        gaB = sb("gaB", [P, B, D])
        sbB = sb("sbB", [P, B, D])
        cbB = sb("cbB", [P, B, D])
        gbB = sb("gbB", [P, B, D])
        gbdiff = sb("gbdiff", [P, D])
        mtmp = sb("mtmp", [P, 2, B, D])
        decay = sb("decay", [P, 5, G])
        bgh = sb("bgh", [P, 2 * G])

        xs = sb("xs", [P, NC, NI, D])
        up = sb("up", [P, G, 3 + T])
        uc = sb("uc", [P, 2, G, TC])
        gg = sb("gg", [P, G, T])
        n1 = sb("n1", [P, NI, D])
        hT = sb("hT", [P, B, TC])
        st = sb("st", [P, 3, NI, 6])
        mv = sb("mv", [P, 3, NI, 2])
        ve = sb("ve", [P, 3, NI])
        rs = sb("rs", [P, 3, NI])
        tf = sb("tf", [P, G, TC])
        ti = sb("ti", [P, G, TC])
        av = sb("av", [P, G, TC])
        bt = sb("bt", [P, G, TC])
        vx = sb("vx", [P, G, TC])
        hh = sb("hh", [P, G, TC])
        hc = sb("hc", [P, G])
        gh = sb("gh", [P, G, TC])
        h2 = sb("h2", [P, NI, D])
        h2T = sb("h2T", [P, NI, P])
        pay = sb("pay", [P, NI, PAY])
        am = sb("am", [P, NI])
        oh = sb("oh", [P, 2, NI, E])
        em = sb("em", [P, NI])
        O = sb("O", [P, B, NC * NJ, E], BF16)

        w2 = up[:, :, :].rearrange("p g t -> p (g t)")[:, 0:E * F]
        b1B = gg[:, :, :].rearrange("p g t -> p (g t)")[:, 0:E * F]

        tot = tf[:, 0, 0:NT * E]
        cum = tf[:, 1, 0:NT * E]
        posb = ti[:, 0, 0:NT * E]
        posO = ti[:, 1, 0:NT * E]
        s8 = sb("s8", [P, 8, E])
        s8i = sb("s8i", [P, 2, E], I32)
        pos = sb("pos", [P, 3, NT])
        posi = sb("posi", [P, 3, NT], I32)
        slotA = sb("slotA", [P, NT, P], BF16)
        pageF = sb("pageF", [P, NT, NP], BF16)
        pageR = sb("pageR", [P, NT, 2, NP], BF16)
        ends = vx[:, 0, 0:NP * E].rearrange("p (n e) -> p n e", e=E)
        val = sb("val", [P, 4, NP])
        gidx = sb("gidx", [P, NP], U32)
        sidx = sb("sidx", [P, NP], U32)
        isb1 = sb("isb1", [P, NP])
        eof = sb("eof", [P, NP])
        eoi = sb("eoi", [P, NP], I32)

        pg = pay[:, 0:RING, :]
        gix = sb("gix", [P, RING], U32)
        six = sb("six", [P, RING], U32)
        og = h2[:, 0:RING, :]
        gs = n1[:, 0:2, :]
        t1 = n1[:, 2:4, :]
        xT = n1[:, 4, :]
        ta = sb("ta", [P, 2])
        al = sb("al", [P, 2])
        hs = h2T[:, 0:FJ, :].rearrange("p j f -> p (j f)")
        hTs = h2T[:, FJ:2 * FJ, :].rearrange("p j f -> p (j f)")

        psT = [ps("psT0"), ps("psT1")]
        psM = [ps(f"psM{g}") for g in range(G)]
        psA = ps("psA")
        psO = [ps("psO0"), ps("psO1")]
        psH, psHT, psY = psM[0], psM[1], [psO[0], psO[1]]

        s_small, s_wmod, s_wi, s_wg, s_wo = sem("small_in"), sem("wmod_in"), sem("wi_in"), sem("wg_in"), sem("wo_in")
        s_x = [sem(f"x{c}_in") for c in range(NC)]
        s_ew, s_out = sem("experts_in"), sem("out_written")
        s_id0, s_const, s_zero, s_iota = sem("ident_zeroed"), sem("ident"), sem("zeroed"), sem("iotas")
        s_cond, s_silu, s_siluB, s_mod, s_modev = sem("cond_tanh"), sem("silu"), sem("siluB"), sem("mod_mm"), sem("mod_copied")
        s_prep, s_dexp, s_decay, s_wog, s_wgd = sem("prep"), sem("decay_exp"), sem("decay"), sem("wo_gated"), sem("wg_diag")
        s_st = [sem(f"ln{n}_stats") for n in range(3)]
        s_mv = [sem(f"ln{n}_mean_var") for n in range(3)]
        s_ve = [sem(f"ln{n}_var_eps") for n in range(3)]
        s_rs = [sem(f"ln{n}_rstd") for n in range(3)]
        s_n1, s_xt, s_hT = sem("n1"), sem("x_turned"), sem("hT")
        s_mm, s_ev = sem("proj_mm"), sem("proj_read")
        s_conv, s_a, s_sq, s_y, s_beta = sem("conv"), sem("alpha"), sem("alpha_sq"), sem("one_less_sq"), sem("beta")
        s_v, s_xin, s_scan, s_carry, s_g = sem("gated_beta"), sem("rec_in"), sem("scan"), sem("carry"), sem("gelu_h")
        s_op, s_x1, s_n2, s_h2m, s_h2 = sem("wo_mm"), sem("x1"), sem("n2"), sem("h2_scaled"), sem("h2")
        s_rm, s_r, s_xn = sem("gb_h2"), sem("resid"), sem("xn")
        s_h2p, s_h2T, s_aff, s_am, s_ar = sem("h2_turned"), sem("h2T"), sem("aff_mm"), sem("aff_max"), sem("aff_read")
        s_rt, s_O, s_row = sem("route_steps"), sem("onehot"), sem("rows_written")
        s_cnt, s_tab, s_tabA, s_idx, s_tabs = sem("counts_mm"), sem("table_steps"), sem("slot_onehots"), sem("index_mm"), sem("tables")
        s_passed = [sem(f"{e}_passed") for e in ("dve", "pool", "sp")]
        s_gix, s_six = sem("gather_index"), sem("scatter_index")
        s_gat = [sem(f"gathered{q}") for q in range(RING)]
        s_sct = [sem(f"scattered{q}") for q in range(RING)]
        s_pt, s_pxT, s_p1, s_ph, s_pht, s_phT, s_p2 = (sem("page_turned"), sem("page_xT"), sem("page_mm1"),
            sem("page_h"), sem("page_h_turned"), sem("page_hT"), sem("page_mm2"))
        s_al, s_t1 = [sem(f"page_alpha{h}") for h in range(2)], [sem(f"page_y{h}") for h in range(2)]
        s_ta, s_gs, s_t2, s_o = sem("page_tanh"), sem("page_gate"), sem("page_yg"), sem("page_out")

        def tm(s):
            return bass.ds(s * TC, TC)

        def experts(eng, k, n):
            return nc.values_load_multi_w_load_instructions(
                eoi[0:1, bass.ds(k, n)], engines=[eng.engine], min_val=0, max_val=E - 1,
                skip_runtime_bounds_check_because="counts are at least 0 and the tables take the minimum with E - 1")[1]

        def bc(ap, n):
            return ap.unsqueeze(1).to_broadcast([P, n, ap.shape[-1]])

        block = ctx.enter_context(nc.Block())

        @block.sync
        def _(sp):
            sp.dma_start(small[:, :], small_d).then_inc(s_small, 16)
            sp.dma_start(wmod[:, :], wmod_d).then_inc(s_wmod, 16)

            def load_x(c):
                for b in range(B):
                    sp.dma_start(xs[:, c, b * NJ:(b + 1) * NJ, :],
                                 x_d[b, c * TC:(c + 1) * TC, :].rearrange("(j p) d -> p j d", p=P)).then_inc(s_x[c], 16)

            load_x(0)
            sp.dma_start(WiT[:, :], WiT_d).then_inc(s_wi, 16)
            sp.dma_start(WgA[:, :], WgT_d[0:P, :]).then_inc(s_wg, 16)
            for b in range(B):
                sp.dma_start(WgH[b * HH:(b + 1) * HH, :], WgT_d[P:HID, :]).then_inc(s_wg, 16)
            sp.dma_start(WoA[:, :], WoT_d[0:P, :]).then_inc(s_wo, 16)
            for b in range(B):
                sp.dma_start(WoH[b * HH:(b + 1) * HH, :], WoT_d[P:HID, :]).then_inc(s_wo, 16)
            for c in range(1, NC):
                load_x(c)
            sp.dma_start(w1[:, :].rearrange("d (e f) -> d e f", e=E), w1_d.rearrange("e d f -> d e f")).then_inc(s_ew, 16)
            sp.dma_start(b2B[:, :], b2_d.partition_broadcast(P)).then_inc(s_ew, 16)

            def store_rows(c):
                ge_apart(sp, s_xn, NI * c + NI, s_passed[2])
                ge_apart(sp, s_r, 2 * c + 2, s_passed[2])
                ge_apart(sp, s_rt, 3 * c + 1, s_passed[2])
                for b in range(B):
                    sp.dma_start(rows_d[bass.ds(b * T + c * TC, TC), :].rearrange("(j p) d -> p j d", p=P),
                                 pay[:, b * NJ:(b + 1) * NJ, :]).then_inc(s_row, 16)

            for c in range(NC - 2):
                store_rows(c)
            sp.wait_ge(s_conv, 12 * NC)
            sp.dma_start(w2.rearrange("p (n d) -> p n d", d=D),
                         w2_d.rearrange("e (j p) d -> p (e j) d", p=P)).then_inc(s_ew, 16)
            sp.wait_ge(s_g, NC)
            sp.dma_start(b1B, b1_d.partition_broadcast(P)).then_inc(s_ew, 16)
            for c in range(NC - 2, NC):
                store_rows(c)
            sp.wait_ge(s_row, 16 * B * NC)

        @block.tensor
        def _(pe):
            pe.wait_ge(s_wmod, 16)
            pe.wait_ge(s_silu, 2)
            for n in range(2):
                mm = pe.matmul(psT[0][:, 2 * n:2 * n + 2], wmod[:, n * D:(n + 1) * D], silu[:, :], start=True, stop=True)
            mm.then_inc(s_mod, 1)
            pe.wait_ge(s_siluB, B)
            for b in range(B):
                pe.matmul(psM[b][:, :], siluB[:, b, :], wmod[:, 2 * D:6 * D], start=True, stop=True).then_inc(s_mod, 1)

            def turn_x(c):
                for b in range(B):
                    ge(pe, s_h2T, 2 * (c - 3) + b + 1)
                    ge(pe, s_n1, NI * c + NJ * (b + 1))
                    if isinstance(c, int) and c == 0:
                        pe.wait_ge(s_modev, 4)
                    for j in range(NJ):
                        mm = pe.transpose(psT[b][:, j * P:(j + 1) * P], n1[:, b * NJ + j, :], ident[:, :])
                    mm.then_inc(s_xt, 1)

            def project(c, k, parts):
                ge(pe, s_ev, NM * c + k - G + 1)
                for out, lhsT, rhs, start, stop in parts:
                    mm = pe.matmul(out, lhsT, rhs, start=start, stop=stop, skip_group_check=True)
                mm.then_inc(s_mm, 1)

            def project_in(c):
                ge(pe, s_hT, 2 * c + 2)
                for k in range(6):
                    ch = HID * (1 - k // 3)
                    ring = psM[k % G]
                    g = k % 3
                    if g < 2:
                        project(c, k, [(ring[:, :], WiT[:, ch:ch + P], hT[:, g, :], True, True)])
                    else:
                        project(c, k, [(ring[b * HH:(b + 1) * HH, :], WiT[:, ch + P:ch + HID], hT[:, b, :], True, True)
                                       for b in range(B)])

            def project_gates(c):
                ge(pe, s_conv, 12 * c + 12)
                for k in range(6, 12):
                    o = HID * ((k - 6) // 3)
                    ring = psM[k % G]
                    g = k % 3
                    if g < 2:
                        half = slice(g * HH, (g + 1) * HH)
                        project(c, k, [(ring[:, :], WgA[:, o:o + P], uc[:, c % 2, g, :], True, False),
                                       (ring[:, :], WgH[half, o:o + P], uc[half, c % 2, 2, :], False, True)])
                    else:
                        project(c, k, [(ring[:, :], WgD[:, (k - 6) // 3, :], uc[:, c % 2, 2, :], True, False)]
                                + [(ring[b * HH:(b + 1) * HH, :], WgA[:, o + P:o + HID], uc[:, c % 2, b, :], False, True)
                                   for b in range(B)])

            def project_out(c):
                ge(pe, s_g, c + 1)
                ge(pe, s_x1, 2 * c)
                for b in range(B):
                    half = slice(b * HH, (b + 1) * HH)
                    for j in range(NJ):
                        out = psO[b][:, j * D:(j + 1) * D]
                        pe.matmul(out, gh[:, b, j * P:(j + 1) * P], WoAg[:, b, :], start=True, stop=False)
                        mm = pe.matmul(out, gh[half, 2, j * P:(j + 1) * P], WoHg[half, :], start=False, stop=True)
                    mm.then_inc(s_op, 1)

            def turn_h2(c):
                for b in range(B):
                    ge(pe, s_h2, 2 * c + b + 1)
                    ge(pe, s_hT, 2 * min(c + 2, NC - 1) + b + 1)
                    for j in range(NJ):
                        mm = pe.transpose(psT[b][:, j * P:(j + 1) * P], h2[:, b * NJ + j, :], ident[:, :])
                    mm.then_inc(s_h2p, 1)

            def affinities(c):
                ge(pe, s_ar, c)
                for b in range(B):
                    ge(pe, s_h2T, 2 * c + b + 1)
                    for j in range(NJ):
                        i = b * NJ + j
                        mm = pe.matmul(psA[:, i * E:(i + 1) * E], h2T[:, i, :], small[:, CENT:CENT + E],
                                       start=True, stop=True)
                mm.then_inc(s_aff, 1)

            pe.wait_ge(s_const, 1)
            pe.wait_ge(s_wi, 16)
            turn_x(0)
            project_in(0)
            pe.wait_ge(s_wg, 48)
            pe.wait_ge(s_wgd, 4)
            project_gates(0)
            for s in range(NC + 2):
                if s < NC:
                    if s:
                        project_gates(s)
                if s >= 2:
                    turn_h2(s - 2)
                if s + 1 < NC:
                    turn_x(s + 1)
                    project_in(s + 1)
                if s >= 2:
                    affinities(s - 2)
                if 1 <= s <= NC:
                    if s == 1:
                        pe.wait_ge(s_wog, 3)
                    project_out(s - 1)

            onehots = O[:, :, :, :].rearrange("p b t e -> p (b t e)")
            pe.wait_ge(s_O, 2 * NC)
            pe.matmul(psM[0][:, 0:NT * E], below[:, :], onehots, start=True, stop=True).then_inc(s_cnt, 1)
            pe.matmul(psM[1][:, 0:NT * E], ones[:, :], onehots, start=True, stop=True).then_inc(s_cnt, 1)
            for t in range(NT):
                if t % 8 == 0:
                    pe.wait_ge(s_tabA, t + 8)
                mm = pe.matmul(psM[2][:, 0:2 * NP], slotA[:, t, :], pageR[:, t, :, :].rearrange("p a n -> p (a n)"),
                               start=(t == 0), stop=(t == NT - 1))
            mm.then_inc(s_idx, 1)

            def turn_page(k, q, lap):
                pe.wait_ge(s_gat[q], 16 * (lap + 1))
                ge(pe, s_pxT, k)
                pe.transpose(psT[0][:, 0:P], pg[:, q, 0:D], ident[:, :]).then_inc(s_pt, 1)

            def up_page(k, e):
                pe.wait_ge(s_pxT, k + 1)
                ge(pe, s_ph, k)
                pe.matmul(psH[:, :], xT, w1[:, bass.ds(e * F, F)], start=True, stop=True).then_inc(s_p1, 1)

            def turn_h(k):
                pe.wait_ge(s_ph, k + 1)
                ge(pe, s_phT, k)
                for j in range(FJ):
                    mm = pe.transpose(psHT[:, j * P:(j + 1) * P], hs[:, j * P:(j + 1) * P], ident[:, :])
                mm.then_inc(s_pht, 1)

            def down_page(k, q, lap, e):
                pe.wait_ge(s_phT, k + 1)
                ge(pe, s_t1[q % 2], HALF * lap + q // 2)
                for j in range(FJ):
                    mm = pe.matmul(psY[q % 2][:, 0:D], hTs[:, j * P:(j + 1) * P], w2[:, bass.ds(e * F + j * D, D)],
                                   start=(j == 0), stop=(j == FJ - 1))
                mm.then_inc(s_p2, 1)

            pe.wait_ge(s_tabs, 3)
            pe.wait_ge(s_ew, 64)
            turn_page(0, 0, 0)
            es = experts(pe, 0, RING + 1)
            up_page(0, es[0])
            turn_page(1, 1, 0)

            def page(k, q, lap, es):
                turn_h(k)
                if not isinstance(k, int) or k + 1 < NP:
                    up_page(k + 1, es[q + 1])
                if not isinstance(k, int) or k + 2 < NP:
                    turn_page(k + 2, (q + 2) % RING, lap + (q + 2) // RING)
                down_page(k, q, lap, es[q])

            for k in range(RING):
                page(k, k, 0, es)
            with pe.Fori(1, NP // RING) as lap:
                es = experts(pe, lap * RING, RING + 1)
                for q in range(RING):
                    page(lap * RING + q, q, lap, es)
            es = experts(pe, NP // RING * RING, NP % RING)
            for k in range(NP // RING * RING, NP):
                page(k, k % RING, k // RING, es)

        @block.scalar
        def _(act):
            act.wait_ge(s_small, 16)
            act.activation(silu[:, :], small[:, COND:COND + B], ACT.Tanh, scale=0.5).then_inc(s_cond, 1)
            act.wait_ge(s_prep, 3)
            act.activation(decay[:, 1, :], decay[:, 0, :], ACT.Exp).then_inc(s_dexp, 1)

            def scale_hT(c):
                for b in range(B):
                    ge(act, s_xt, 2 * c + b + 1)
                    ge(act, s_mm, NM * (c - 1) + 6)
                    act.activation(hT[:, b, :], psT[b][:, :], ACT.Identity, bias=modT[:, b:b + 1],
                                   scale=modT[:, 2 + b:3 + b]).then_inc(s_hT, 1)

            def read_in(c):
                for g in range(G):
                    ge(act, s_mm, NM * c + g + 1)
                    act.activation(up[:, g, bass.ds(c * TC + 3, TC)], psM[g][:, :], ACT.Copy).then_inc(s_ev, 1)
                for g in range(G):
                    ge(act, s_mm, NM * c + 3 + g + 1)
                    act.activation(gg[:, g, tm(c)], psM[g][:, :], ACT.Gelu).then_inc(s_ev, 1)

            def read_gates(c):
                for k in range(6, 12):
                    g = k % 3
                    ge(act, s_mm, NM * c + k + 1)
                    if k == 9:
                        ge(act, s_v, c)
                    act.activation((tf if k < 9 else ti)[:, g, :], psM[k % G][:, :], ACT.Tanh,
                                   bias=bgh[:, k - 6:k - 5], scale=0.5).then_inc(s_ev, 1)

            def alpha(c):
                ge(act, s_scan, 3 * c)
                for g in range(G):
                    ge(act, s_ev, NM * c + 7 + g)
                    act.activation(av[:, g, :], tf[:, g, :], ACT.Exp, bias=decay[:, 4, g:g + 1],
                                   scale=decay[:, 4, g:g + 1]).then_inc(s_a, 1)
                ge(act, s_a, 3 * c + 3)
                act.activation(tf[:, :, :], av[:, :, :], ACT.Square).then_inc(s_sq, 1)

            def beta(c):
                ge(act, s_y, c + 1)
                act.activation(bt[:, :, :], bt[:, :, :], ACT.Sqrt, bias=epsc[:, :]).then_inc(s_beta, 1)

            def copy_h2T(c):
                for b in range(B):
                    ge(act, s_h2p, 2 * c + b + 1)
                    ge(act, s_aff, c)
                    act.activation(h2T[:, b * NJ:(b + 1) * NJ, :].rearrange("p j t -> p (j t)"), psT[b][:, :],
                                   ACT.Copy).then_inc(s_h2T, 1)

            act.wait_ge(s_modev, 2)
            scale_hT(0)
            act.wait_ge(s_zero, 1)
            read_in(0)
            act.wait_ge(s_prep, 5)
            for s in range(NC + 2):
                if s < NC:
                    read_gates(s)
                if s >= 2:
                    copy_h2T(s - 2)
                if s + 1 < NC:
                    scale_hT(s + 1)
                if s < NC:
                    if s == 0:
                        act.wait_ge(s_decay, 8)
                        act.wait_ge(s_iota, 1)
                    alpha(s)
                    beta(s)
                if s + 1 < NC:
                    read_in(s + 1)

            def scale_page(k, e):
                act.wait_ge(s_pt, k + 1)
                ge(act, s_p1, k)
                act.activation(xT, psT[0][:, 0:P], ACT.Identity, bias=small[:, bass.ds(LN_B + e, 1)],
                               scale=small[:, bass.ds(LN_G + e, 1)]).then_inc(s_pxT, 1)

            def page(k, q, lap, es):
                act.wait_ge(s_pht, k + 1)
                ge(act, s_p2, k)
                act.activation(hTs, psHT[:, :], ACT.Relu).then_inc(s_phT, 1)
                if not isinstance(k, int) or k + 2 < NP:
                    scale_page(k + 2, es[q + 2])
                act.wait_ge(s_gat[q], 16 * (lap + 1))
                ge(act, s_al[q % 2], HALF * lap + q // 2)
                act.activation(ta[:, q % 2:q % 2 + 1], pg[:, q, 2 * D:2 * D + 1], ACT.Tanh, scale=0.5).then_inc(s_ta, 1)

            act.wait_ge(s_tabs, 3)
            es = experts(act, 0, RING + 2)
            scale_page(0, es[0])
            scale_page(1, es[1])
            for k in range(RING):
                page(k, k, 0, es)
            with act.Fori(1, NP // RING) as lap:
                es = experts(act, lap * RING, RING + 2)
                for q in range(RING):
                    page(lap * RING + q, q, lap, es)
            es = experts(act, NP // RING * RING, NP % RING)
            for k in range(NP // RING * RING, NP):
                page(k, k % RING, k // RING, es)

        @block.vector
        def _(dve):
            v = dve
            steps = [0]

            def prep(ins):
                ins.then_inc(s_prep, 1)
                steps[0] += 1
                v.wait_ge(s_prep, steps[0])

            v.wait_ge(s_small, 16)
            prep(v.tensor_scalar(decay[:, 0, :], small[:, FORGET:FORGET + G], -1.0, None, ALU.mult))
            prep(v.tensor_tensor(decay[:, 3, :], small[:, FORGET:FORGET + G], decay[:, 0, :], ALU.max))
            prep(v.tensor_scalar(decay[:, 0, :], decay[:, 3, :], -1.0, None, ALU.mult))
            prep(v.tensor_scalar(bgh[:, :], small[:, BG_F:BG_F + 2 * G], 0.5, None, ALU.mult))
            prep(v.tensor_scalar(decay[:, 3, :], small[:, FORGET:FORGET + G], 0.0, -4.0, ALU.max, ALU.mult))
            v.wait_ge(s_cond, 1)
            v.scalar_tensor_tensor(out=silu[:, :], in0=silu[:, :], scalar=1.0, in1=small[:, COND:COND + B],
                                   op0=ALU.add, op1=ALU.mult).then_inc(s_silu, 1)
            v.wait_ge(s_silu, 1)
            v.tensor_scalar(silu[:, :], silu[:, :], 0.5, None, ALU.mult).then_inc(s_silu, 1)
            v.wait_ge(s_silu, 2)
            v.wait_ge(s_iota, 1)
            for b in range(B):
                v.tensor_scalar(siluB[:, b, :], iotaS[:, :], 0.0, silu[:, b:b + 1], ALU.mult,
                                ALU.add).then_inc(s_siluB, 1)
            v.wait_ge(s_mod, 1)
            v.tensor_copy(modT[:, 0:2], psT[0][:, 0:2]).then_inc(s_modev, 1)
            v.tensor_scalar(modT[:, 2:4], psT[0][:, 2:4], 1.0, None, ALU.add).then_inc(s_modev, 1)

            def ln_stats(n, c, tile):
                for i in range(NI):
                    v.bn_stats(st[:, n, i, :], tile(i)).then_inc(s_st[n], 1)
                ge_apart(v, s_st[n], NI * c + NI, s_passed[0])
                for i in range(NI):
                    v.bn_aggr(mv[:, n, i, :], st[:, n, i, :]).then_inc(s_mv[n], 1)

            def ln_out(n, c, tile, out, done):
                ge(v, s_rs[n], c + 1)
                for i in range(NI):
                    v.tensor_scalar(out(i), tile(i), mv[:, n, i, 0:1], rs[:, n, i:i + 1], ALU.subtract,
                                    ALU.mult).then_inc(done, 1)

            def conv(c):
                ge(v, s_ev, NM * c + 3)
                for g in range(G):
                    v.tensor_scalar(uc[:, c % 2, g, :], up[:, g, bass.ds(c * TC + 3, TC)],
                                    small[:, CONV_W + 9 + g:CONV_W + 10 + g], small[:, CONV_B + g:CONV_B + g + 1],
                                    ALU.mult, ALU.add).then_inc(s_conv, 1)
                for n in range(1, 4):
                    for g in range(G):
                        ge(v, s_conv, 12 * c + 3 * n + g - 2)
                        w = CONV_W + 3 * (3 - n) + g
                        v.scalar_tensor_tensor(out=uc[:, c % 2, g, :], in0=up[:, g, bass.ds(c * TC + 3 - n, TC)],
                                               scalar=small[:, w:w + 1], in1=uc[:, c % 2, g, :], op0=ALU.mult,
                                               op1=ALU.add).then_inc(s_conv, 1)

            def residual(c):
                for b in range(B):
                    ge(v, s_op, 2 * c + b + 1)
                    xb = xs[:, c, b * NJ:(b + 1) * NJ, :].rearrange("p j d -> p (j d)")
                    v.tensor_tensor(xb, xb, psO[b][:, :], ALU.add).then_inc(s_x1, 1)
                v.wait_ge(s_x1, 2 * c + 2)

            def modulated(c):
                ge(v, s_h2p, 2 * c)
                ge(v, s_rm, 2 * c)
                ln_out(1, c, lambda i: xs[:, c, i, :], lambda i: h2[:, i, :], s_n2)

            def shifted(c):
                for b in range(B):
                    ge(v, s_h2m, 2 * c + b + 1)
                    hb = h2[:, b * NJ:(b + 1) * NJ, :]
                    v.tensor_tensor(hb, hb, bc(sbB[:, b, :], NJ), ALU.add).then_inc(s_h2, 1)
                ge(v, s_h2, 2 * c + 2)
                ln_stats(2, c, lambda i: h2[:, i, :])

            def rows(c):
                ge(v, s_row, 16 * B * c)
                ln_out(2, c, lambda i: h2[:, i, :], lambda i: pay[:, i, 0:D], s_xn)
                for b in range(B):
                    ge(v, s_rm, 2 * c + b + 1)
                    rb = pay[:, b * NJ:(b + 1) * NJ, D:2 * D]
                    v.tensor_tensor(rb, rb, xs[:, c, b * NJ:(b + 1) * NJ, :], ALU.add).then_inc(s_r, 1)

            def gate_input(c):
                ge(v, s_beta, c + 1)
                v.scalar_tensor_tensor(out=vx[:, :, :], in0=ti[:, :, :], scalar=1.0, in1=bt[:, :, :],
                                       op0=ALU.add, op1=ALU.mult).then_inc(s_v, 1)

            def recur(c):
                ge(v, s_xin, c + 1)
                ge(v, s_g, c)
                for g in range(G):
                    if isinstance(c, int) and c == 0:
                        first = 0.0
                    else:
                        first = hc[:, g:g + 1]
                        if g == 0:
                            ge(v, s_carry, c)
                    v.tensor_tensor_scan(hh[:, g, :], av[:, g, :], vx[:, g, :], first, ALU.mult,
                                         ALU.add).then_inc(s_scan, 1)
                ge(v, s_scan, 3 * c + 3)
                v.tensor_copy(hc[:, :], hh[:, :, TC - 1]).then_inc(s_carry, 1)

            def route(c):
                ge(v, s_aff, c + 1)
                aff = psA[:, 0:NI * E].rearrange("p (i e) -> p i e", e=E)
                v.tensor_reduce(am[:, :], aff, AX.X, ALU.max).then_inc(s_am, 1)
                ge(v, s_am, c + 1)
                v.tensor_copy(pay[:, :, 2 * D], am[:, :]).then_inc(s_rt, 1)
                v.tensor_tensor(oh[:, 0, :, :], aff, am[:, :].unsqueeze(2).to_broadcast([P, NI, E]),
                                ALU.is_equal).then_inc(s_ar, 1)
                ge(v, s_ar, c + 1)
                v.tensor_tensor(oh[:, 1, :, :], oh[:, 0, :, :], bc(iotaE[:, :], NI), ALU.mult).then_inc(s_rt, 1)
                ge(v, s_rt, 3 * c + 2)
                v.tensor_reduce(em[:, :], oh[:, 1, :, :], AX.X, ALU.min).then_inc(s_rt, 1)
                ge(v, s_rt, 3 * c + 3)
                for b in range(B):
                    v.tensor_tensor(O[:, b, bass.ds(c * NJ, NJ), :], bc(iotaE[:, :], NJ),
                                    em[:, b * NJ:(b + 1) * NJ].unsqueeze(2).to_broadcast([P, NJ, E]),
                                    ALU.is_equal).then_inc(s_O, 1)

            v.wait_ge(s_x[0], 32)
            ln_stats(0, 0, lambda i: xs[:, 0, i, :])
            ln_out(0, 0, lambda i: xs[:, 0, i, :], lambda i: n1[:, i, :], s_n1)

            v.wait_ge(s_wg, 48)
            v.wait_ge(s_zero, 1)
            for n in range(2):
                o = HID * n + P
                for b in range(B):
                    half = slice(b * HH, (b + 1) * HH)
                    v.tensor_copy(WgD[half, n, half], WgH[half, o:o + HH]).then_inc(s_wgd, 1)

            for b in range(B):
                v.wait_ge(s_mod, 2 + b)
                prep(v.tensor_copy(gaB[:, b, :], psM[b][:, 0:D]))
                prep(v.tensor_copy(sbB[:, b, :], psM[b][:, D:2 * D]))
                prep(v.tensor_scalar(cbB[:, b, :], psM[b][:, 2 * D:3 * D], 1.0, None, ALU.add))
                v.tensor_copy(gbB[:, b, :], psM[b][:, 3 * D:4 * D]).then_inc(s_modev, 1)
            conv(0)
            v.wait_ge(s_modev, 2 + B)
            for gate in (gaB, gbB):
                prep(v.tensor_scalar(mtmp[:, 0, :, :], gate[:, :, :], -1.0, None, ALU.mult))
                prep(v.tensor_tensor(mtmp[:, 0, :, :], mtmp[:, 0, :, :], gate[:, :, :], ALU.max))
                prep(v.tensor_scalar(mtmp[:, 0, :, :], mtmp[:, 0, :, :], 0.25, None, ALU.max))
                prep(v.tensor_scalar(mtmp[:, 1, :, :], gate[:, :, :], 0.0, 2.0, ALU.is_ge, ALU.mult))
                prep(v.scalar_tensor_tensor(out=gate[:, :, :], in0=mtmp[:, 1, :, :], scalar=-1.0,
                                            in1=mtmp[:, 0, :, :], op0=ALU.add, op1=ALU.mult))
            prep(v.tensor_tensor(gbdiff[:, :], gbB[:, 1, :], gbB[:, 0, :], ALU.subtract))
            v.wait_ge(s_wo, 48)
            v.scalar_tensor_tensor(out=WoAg[:, :, :], in0=gaB[:, :, :], scalar=0.5, in1=bc(WoA[:, :], B),
                                   op0=ALU.mult, op1=ALU.mult).then_inc(s_wog, 1)
            for b in range(B):
                half = slice(b * HH, (b + 1) * HH)
                v.scalar_tensor_tensor(out=WoHg[half, :], in0=WoH[half, :], scalar=0.5, in1=gaB[half, b, :],
                                       op0=ALU.mult, op1=ALU.mult).then_inc(s_wog, 1)
            v.wait_ge(s_dexp, 1)
            z, s, s2, acc = decay[:, 1, :], decay[:, 0, :], decay[:, 2, :], decay[:, 4, :]
            prep(v.tensor_scalar(s2, z, 2.0, None, ALU.add))
            prep(v.reciprocal(s2, s2))
            prep(v.tensor_tensor(s, z, s2, ALU.mult))
            prep(v.tensor_tensor(s2, s, s, ALU.mult))
            prep(v.tensor_scalar(acc, s2, 1.0 / 17, 1.0 / 15, ALU.mult, ALU.add))
            done = 0
            for n in (13, 11, 9, 7, 5, 3, 1):
                v.tensor_tensor(acc, acc, s2, ALU.mult).then_inc(s_decay, 1)
                done += 1
                v.wait_ge(s_decay, done)
                prep(v.tensor_scalar(acc, acc, 1.0 / n, None, ALU.add))
            prep(v.tensor_tensor(acc, acc, s, ALU.mult))
            v.scalar_tensor_tensor(out=acc, in0=acc, scalar=-8.0, in1=decay[:, 3, :], op0=ALU.mult,
                                   op1=ALU.add).then_inc(s_decay, 1)

            for s in range(NC + 2):
                ahead = lambda i: xs[:, s + 1, i, :]
                behind = lambda i: xs[:, s - 2, i, :]
                if s >= 2:
                    residual(s - 2)
                    ln_stats(1, s - 2, behind)
                if s + 1 < NC:
                    v.wait_ge(s_x[s + 1], 32)
                    ln_stats(0, s + 1, ahead)
                if s >= 2:
                    modulated(s - 2)
                if s + 1 < NC:
                    ge(v, s_xt, 2 * (s + 1))
                    ln_out(0, s + 1, ahead, lambda i: n1[:, i, :], s_n1)
                if s >= 2:
                    shifted(s - 2)
                    rows(s - 2)
                if s < NC:
                    gate_input(s)
                if s + 1 < NC:
                    conv(s + 1)
                if s < NC:
                    recur(s)
                if s >= 2:
                    route(s - 2)

            tb = [0]

            def tab(ins):
                ins.then_inc(s_tab, 1)
                tb[0] += 1
                v.wait_ge(s_tab, tb[0])

            def et(ap):
                return ap.rearrange("p (e t) -> p e t", e=E)

            def te(ap):
                return ap.rearrange("p (t e) -> p e t", e=E)

            v.wait_ge(s_cnt, 2)
            v.wait_ge(s_iota, 2)
            tab(v.tensor_copy(et(tot), te(psM[1][:, 0:NT * E])))
            tab(v.tensor_tensor_scan(cum, onesf[:, :], tot, 0.0, ALU.mult, ALU.add))
            end = cum.rearrange("p (e t) -> p e t", e=E)[:, :, NT - 1]
            count, pages, pend, shift, low = (s8[:, n, :] for n in range(5))
            v.tensor_copy(low[:, 1:E], end[:, 0:E - 1]).then_inc(s_tab, 1)
            tab(v.memset(low[:, 0:1], 0.0))
            tb[0] += 1
            v.wait_ge(s_tab, tb[0])
            tab(v.tensor_tensor(count, end, low, ALU.subtract))
            tab(v.tensor_scalar(s8i[:, 0, :], count, float(P - 1), None, ALU.add))
            tab(v.tensor_scalar(s8i[:, 1, :], s8i[:, 0, :], 7, None, ALU.logical_shift_right))
            tab(v.tensor_copy(pages, s8i[:, 1, :]))
            tab(v.tensor_tensor_scan(pend, onesf[:, 0:E], pages, 0.0, ALU.mult, ALU.add))
            tab(v.tensor_tensor(shift, pend, pages, ALU.subtract))
            tab(v.scalar_tensor_tensor(out=shift, in0=shift, scalar=float(P), in1=low, op0=ALU.mult, op1=ALU.subtract))
            tab(v.tensor_tensor(posb, cum, tot, ALU.subtract))
            tab(v.tensor_tensor(et(posb), et(posb), shift.unsqueeze(2).to_broadcast([P, E, NT]), ALU.add))
            tab(v.tensor_tensor(et(posb), et(posb), te(psM[0][:, 0:NT * E]), ALU.add))
            tab(v.tensor_tensor(et(posO), et(posb), te(O[:, :, :, :].rearrange("p b t e -> p (b t e)")), ALU.mult))
            tab(v.tensor_reduce(pos[:, 0, :], posO.rearrange("p (e t) -> p t e", e=E), AX.X, ALU.add))
            tab(v.tensor_copy(posi[:, 0, :], pos[:, 0, :]))
            tab(v.tensor_scalar(posi[:, 1, :], posi[:, 0, :], 7, None, ALU.logical_shift_right))
            tab(v.tensor_scalar(posi[:, 2, :], posi[:, 0, :], P - 1, None, ALU.bitwise_and))
            tab(v.tensor_copy(pos[:, 1:3, :], posi[:, 1:3, :]))
            tab(v.tensor_tensor(pageF[:, :, :], bc(iotaP[:, :], NT),
                                pos[:, 1, :].unsqueeze(2).to_broadcast([P, NT, NP]), ALU.is_equal))
            tab(v.tensor_scalar(pageR[:, :, 0, :], pageF[:, :, :], part1[:, :], None, ALU.mult))
            tab(v.tensor_tensor(pageR[:, :, 1, :], pageF[:, :, :],
                                iotaT[:, :].unsqueeze(2).to_broadcast([P, NT, NP]), ALU.mult))
            for t in range(NT):
                v.tensor_scalar(slotA[:, t, :], iotaS[:, :], pos[:, 2, t:t + 1], None, ALU.is_equal).then_inc(s_tabA, 1)
            tab(v.tensor_tensor(ends, iotaP[:, :].unsqueeze(2).to_broadcast([P, NP, E]),
                                pend.unsqueeze(1).to_broadcast([P, NP, E]), ALU.is_ge))
            tab(v.tensor_reduce(eof[:, :], ends, AX.X, ALU.add))
            tab(v.tensor_scalar(eof[:, :], eof[:, :], float(E - 1), None, ALU.min))
            v.tensor_copy(eoi[:, :], eof[:, :]).then_inc(s_tabs, 1)
            v.wait_ge(s_idx, 1)
            tab(v.tensor_copy(val[:, 0, :], psM[2][:, 0:NP]))
            tab(v.scalar_tensor_tensor(out=val[:, 1, :], in0=psM[2][:, NP:2 * NP], scalar=float(P), in1=val[:, 0, :],
                                       op0=ALU.mult, op1=ALU.add))
            tab(v.tensor_scalar(val[:, 2, :], val[:, 1, :], -1.0, 0.0, ALU.add, ALU.max))
            v.tensor_copy(gidx[:, :], val[:, 2, :]).then_inc(s_tabs, 1)
            tab(v.tensor_scalar(val[:, 3, :], val[:, 1, :], 0.0, float(2 * B * T), ALU.is_equal, ALU.mult))
            tab(v.tensor_tensor(val[:, 3, :], val[:, 3, :], val[:, 2, :], ALU.add))
            tab(v.tensor_scalar(isb1[:, :], val[:, 2, :], float(T), None, ALU.is_ge))
            v.tensor_copy(sidx[:, :], val[:, 3, :]).then_inc(s_tabs, 1)

            def bias_h(k, e):
                v.wait_ge(s_p1, k + 1)
                ge(v, s_pht, k)
                v.tensor_tensor(hs, psH[:, :], b1B[:, bass.ds(e * F, F)], ALU.add).then_inc(s_ph, 1)

            def page(k, q, lap, es):
                if not isinstance(k, int) or k + 1 < NP:
                    bias_h(k + 1, es[q + 1])
                two = q % 2
                v.tensor_scalar(gs[:, two, :], gbdiff[:, :], isb1[:, bass.ds(k, 1)], None, ALU.mult).then_inc(s_gs, 1)
                v.wait_ge(s_ta, k + 1)
                v.tensor_scalar(al[:, two:two + 1], ta[:, two:two + 1], 1.0, 0.5, ALU.add, ALU.mult).then_inc(s_al[two], 1)
                v.wait_ge(s_gs, 2 * k + 1)
                v.tensor_tensor(gs[:, two, :], gs[:, two, :], gbB[:, 0, :], ALU.add).then_inc(s_gs, 1)
                e = es[q]
                v.wait_ge(s_p2, k + 1)
                v.tensor_tensor(t1[:, two, :], psY[two][:, 0:D], b2B[:, bass.ds(e * D, D)], ALU.add).then_inc(s_t1[two], 1)
                v.wait_ge(s_t1[two], HALF * lap + q // 2 + 1)
                v.wait_ge(s_gs, 2 * k + 2)
                v.wait_ge(s_al[two], HALF * lap + q // 2 + 1)
                v.scalar_tensor_tensor(out=t1[:, two, :], in0=t1[:, two, :], scalar=al[:, two:two + 1],
                                       in1=gs[:, two, :], op0=ALU.mult, op1=ALU.mult).then_inc(s_t2, 1)
                v.wait_ge(s_t2, k + 1)
                ge(v, s_sct[q], 16 * lap)
                v.wait_ge(s_gat[q], 16 * (lap + 1))
                v.tensor_tensor(og[:, q, :], t1[:, two, :], pg[:, q, D:2 * D], ALU.add).then_inc(s_o, 1)

            v.wait_ge(s_tabs, 3)
            v.wait_ge(s_ew, 64)
            es = experts(v, 0, RING + 1)
            bias_h(0, es[0])
            for k in range(RING):
                page(k, k, 0, es)
            with v.Fori(1, NP // RING) as lap:
                es = experts(v, lap * RING, RING + 1)
                for q in range(RING):
                    page(lap * RING + q, q, lap, es)
            es = experts(v, NP // RING * RING, NP % RING)
            for k in range(NP // RING * RING, NP):
                page(k, k % RING, k // RING, es)

        @block.gpsimd
        def _(pool):
            g = pool
            g.memset(ident[:, :], 0.0).then_inc(s_id0, 1)
            g.memset(below[:, :], 1.0)
            g.memset(up[:, :, 0:3], 0.0)
            g.memset(WgD[:, :, :], 0.0).then_inc(s_zero, 1)
            g.memset(ones[:, :], 1.0)
            g.iota(iotaS[:, :], pattern=[[1, P]], base=0, channel_multiplier=0, allow_small_or_imprecise_dtypes=True)
            g.memset(epsc[:, :], 1e-6)
            g.memset(mhalf[:, :], -0.5).then_inc(s_iota, 1)
            g.wait_ge(s_id0, 1)
            g.affine_select(out=ident[:, :], in_=ident[:, :], compare_op=ALU.not_equal, fill=1.0, base=0,
                            pattern=[[-1, P]], channel_multiplier=1).then_inc(s_const, 1)

            def rstd(n, c):
                ge_apart(g, s_mv[n], NI * c + NI, s_passed[1])
                g.tensor_scalar(ve[:, n, :], mv[:, n, :, 1], EPS, None, ALU.add).then_inc(s_ve[n], 1)
                ge(g, s_ve[n], c + 1)
                g.tensor_tensor(rs[:, n, :], ve[:, n, :], mhalf[:, :], ALU.pow).then_inc(s_rs[n], 1)

            def modulate(c):
                for b in range(B):
                    ge(g, s_n2, NI * c + NJ * (b + 1))
                    hb = h2[:, b * NJ:(b + 1) * NJ, :]
                    g.tensor_tensor(hb, hb, bc(cbB[:, b, :], NJ), ALU.mult).then_inc(s_h2m, 1)
                ge(g, s_row, 16 * B * c)
                rstd(2, c)
                for b in range(B):
                    ge(g, s_h2, 2 * c + b + 1)
                    g.tensor_tensor(pay[:, b * NJ:(b + 1) * NJ, D:2 * D], h2[:, b * NJ:(b + 1) * NJ, :],
                                    bc(gbB[:, b, :], NJ), ALU.mult).then_inc(s_rm, 1)

            def recur(c):
                ge(g, s_sq, c + 1)
                ge_apart(g, s_v, c, s_passed[1])
                g.tensor_scalar(bt[:, :, :], tf[:, :, :], -1.0, 1.0, ALU.mult, ALU.add).then_inc(s_y, 1)
                ge(g, s_v, c + 1)
                g.tensor_tensor(vx[:, :, :], vx[:, :, :], uc[:, c % 2, :, :], ALU.mult).then_inc(s_xin, 1)
                ge(g, s_scan, 3 * c + 3)
                ge(g, s_op, 2 * c)
                g.tensor_tensor(gh[:, :, :], gg[:, :, tm(c)], hh[:, :, :], ALU.mult).then_inc(s_g, 1)

            rstd(0, 0)
            g.wait_ge(s_zero, 1)
            g.affine_select(out=below[:, :], in_=below[:, :], compare_op=ALU.is_gt, fill=0.0, base=0,
                            pattern=[[1, P]], channel_multiplier=-1)
            g.memset(pay[:, :, 2 * D + 1:PAY], 0.0)
            g.iota(iotaE[:, :], pattern=[[1, E]], base=-E, channel_multiplier=0, allow_small_or_imprecise_dtypes=True)
            g.iota(iotaP[:, :], pattern=[[1, NP]], base=0, channel_multiplier=0, allow_small_or_imprecise_dtypes=True)
            g.iota(iotaT[:, :], pattern=[[1, NT]], base=0, channel_multiplier=0, allow_small_or_imprecise_dtypes=True)
            g.iota(part1[:, :], pattern=[[0, 1]], base=1, channel_multiplier=1, allow_small_or_imprecise_dtypes=True)
            g.memset(onesf[:, :], 1.0).then_inc(s_iota, 1)
            for s in range(NC + 2):
                if s >= 2:
                    rstd(1, s - 2)
                if s + 1 < NC:
                    rstd(0, s + 1)
                if s >= 2:
                    modulate(s - 2)
                if s < NC:
                    recur(s)

            def gather(k, q):
                g.tensor_copy(gix[:, q:q + 1], gidx[:, bass.ds(k, 1)]).then_inc(s_gix, 1)
                ge_apart(g, s_gix, k + 1, s_passed[1])
                g.indirect_dma_start(out=pg[:, q, :], out_offset=None, in_=rows_d,
                                     in_offset=bass.IndirectOffsetOnAxis(ap=gix[:, q:q + 1], axis=0)).then_inc(s_gat[q], 16)

            def scatter(k, q):
                g.tensor_copy(six[:, q:q + 1], sidx[:, bass.ds(k, 1)]).then_inc(s_six, 1)
                g.wait_ge(s_six, k + 1)
                ge_apart(g, s_o, k + 1, s_passed[1])
                g.indirect_dma_start(out=out_d, out_offset=bass.IndirectOffsetOnAxis(ap=six[:, q:q + 1], axis=0),
                                     in_=og[:, q, :], in_offset=None, bounds_check=B * T - 1,
                                     oob_is_err=False).then_inc(s_sct[q], 16)

            g.wait_ge(s_tabs, 3)
            g.wait_ge(s_row, 16 * B * NC)
            for k in range(RING):
                gather(k, k)
            with g.Fori(0, NP // RING - 1) as lap:
                for q in range(RING):
                    scatter(lap * RING + q, q)
                    gather(lap * RING + RING + q, q)
            for k in range(NP // RING * RING - RING, NP):
                scatter(k, k % RING)
                if k + RING < NP:
                    gather(k + RING, k % RING)
            for q in range(RING):
                g.wait_ge(s_sct[q], 16 * len(range(q, NP, RING)))


def kernel(**inputs):
    import numpy as _np
    import concourse.bacc as _bacc
    from concourse.bass_utils import run_bass_kernel_spmd as _run

    a = {n: _np.asarray(v) for n, v in inputs.items()}

    def groups(v):
        return _np.stack([v[:P], v[:P], _np.concatenate([v[P:], v[P:]])], axis=1)

    H = a["L0_attn_Wg"].shape[1]
    bg = a["L0_attn_bg"]
    cw = a["L0_attn_conv_w"][:, 0, :]
    small = _np.concatenate(
        [groups(a["L0_attn_conv_b"]), groups(bg[:H]), groups(bg[H:]), groups(a["L0_attn_forget_base"])]
        + [groups(cw[:, k]) for k in range(cw.shape[1])]
        + [a["L0_ffn_ln_g"].T, a["L0_ffn_ln_b"].T, a["L0_c"].T, a["L0_ffn_centroids"].T], axis=1)
    arrays = {
        "x": a["L0_attn_x"], "WiT": a["L0_attn_Wi"].T, "WgT": a["L0_attn_Wg"].T, "WoT": a["L0_attn_Wo"].T,
        "small": small, "w1": a["L0_ffn_w1"], "b1": a["L0_ffn_b1"].reshape(-1), "w2": a["L0_ffn_w2"],
        "b2": a["L0_ffn_b2"].reshape(-1), "wmod": a["L0_wmod"],
    }
    nc = _bacc.Bacc("TRN2", target_bir_lowering=False, num_devices=1)
    arrays = {f"in_{n}": _np.ascontiguousarray(v) for n, v in arrays.items()}
    args = [nc.dram_tensor(n, v.shape, mybir.dt.from_np(v.dtype), kind="ExternalInput").ap() for n, v in arrays.items()]
    shape = a["L0_attn_x"].shape
    out = nc.dram_tensor("out", (shape[0] * shape[1], shape[2]), F32, kind="ExternalOutput").ap()
    adaln_block_kernel(nc, *args, out)
    r = _run(nc, [arrays], core_ids=[0])
    return r.results[0]["out"].reshape(shape)
```

```python
from contextlib import ExitStack

import concourse.bass as bass
from concourse import mybir

ALU = mybir.AluOpType
ACT = mybir.ActivationFunctionType
AX = mybir.AxisListType
F32 = mybir.dt.float32
BF16 = mybir.dt.bfloat16
I32 = mybir.dt.int32
U32 = mybir.dt.uint32

P = 128
EPS = 1e-5

CONV_B, BG_F, BG_I, FORGET, CONV_W, LN_G, LN_B, COND, CENT, B1, SMALL = 0, 3, 6, 9, 12, 24, 32, 40, 42, 50, 82


def ge(eng, sem, value):
    if isinstance(value, int) and value <= 0:
        return
    eng.wait_ge(sem, value)


def ge_apart(eng, sem, value, passed):
    ge(eng, sem, value)
    if not isinstance(value, int):
        eng.sem_inc(passed, 1)


def adaln_block_kernel(nc, x_d, WiT_d, WgT_d, WoT_d, small_d, w1_d, w2_d, b2_d, wmod_d, out_d):
    B, T, D = x_d.shape
    HID = WgT_d.shape[0]
    E, _, F = w1_d.shape
    TC = 256
    NC = T // TC
    NJ = TC // P
    NI = B * NJ
    NT = B * T // P
    HH = HID - P
    FJ = F // P
    G = 3
    NP = NT + E - 1
    RING = 6
    HALF = RING // 2
    PAY = 2 * D + 4
    REG = B * T + P
    NM = 4 * G
    assert B == 2 and HH == 64 and D == P and T % TC == 0 and (NP - 3) % RING == 0

    ctx = ExitStack()
    with ctx:
        def sb(name, shape, dt=F32):
            return ctx.enter_context(nc.sbuf_tensor(name, shape, dt))

        def ps(name):
            return ctx.enter_context(nc.psum_tensor(name, [P, 512], F32))

        def sem(name):
            return ctx.enter_context(nc.semaphore(name))

        rows_d = nc.dram_tensor("rows_d", [E * REG + (E - 1) * P, PAY], F32, kind="Internal").ap()

        WiT = sb("WiT", [P, 2 * HID])
        WgA = sb("WgA", [P, 2 * HID])
        WgH = sb("WgH", [P, 2 * HID])
        WgD = sb("WgD", [P, 2, P])
        WoA = sb("WoA", [P, D])
        WoH = sb("WoH", [P, D])
        WoAg = sb("WoAg", [P, B, D])
        WoHg = sb("WoHg", [P, D])
        small = sb("small", [P, SMALL])
        wmod = sb("wmod", [P, 6 * D])
        w1 = sb("w1", [P, E * F])
        b2B = sb("b2B", [P, E * D])
        ident = sb("ident", [P, P])
        below = sb("below", [P, P], BF16)
        ones = sb("ones", [P, P], BF16)
        onesf = sb("onesf", [P, E])
        iotaE = sb("iotaE", [P, E])
        iotaP = sb("iotaP", [P, NP])
        zeros = sb("zeros", [P, P])
        empty = sb("empty", [P, PAY])
        epsc = sb("epsc", [P, 1])
        mhalf = sb("mhalf", [P, NI])

        silu = sb("silu", [P, B])
        siluB = sb("siluB", [P, B, P])
        modT = sb("modT", [P, 4])
        modB = sb("modB", [P, B, 4, D])
        gaB, sbB, cbB, gbB = (modB[:, :, n, :] for n in range(4))
        gbdiff = sb("gbdiff", [P, D])
        mtmp = sb("mtmp", [P, 2, 2, B, D])
        decay = sb("decay", [P, 5, G])
        bgh = sb("bgh", [P, 2 * G])

        xs = sb("xs", [P, NC, NI, D])
        up = sb("up", [P, G, 3 + T])
        uc = sb("uc", [P, 3, G, TC])
        gg = sb("gg", [P, G, T])
        n1 = sb("n1", [P, NI, D])
        hT = sb("hT", [P, B, TC])
        st = sb("st", [P, 3, NI, 6])
        mv = sb("mv", [P, 3, NI, 2])
        ve = sb("ve", [P, 3, NI])
        rs = sb("rs", [P, 3, NI])
        tf = sb("tf", [P, G, TC])
        ti = sb("ti", [P, G, TC])
        av = sb("av", [P, G, TC])
        bt = sb("bt", [P, G, TC])
        vx = sb("vx", [P, G, TC])
        hh = sb("hh", [P, G, TC])
        hc = sb("hc", [P, G])
        gh = sb("gh", [P, G, TC])
        h2 = sb("h2", [P, 2, NI, D])
        h2T = sb("h2T", [P, NI, P])
        pay = sb("pay", [P, 2, NI, PAY])
        am = sb("am", [P, NI])
        oh = sb("oh", [P, 2, NI, E])
        em = sb("em", [P, NI])
        O = sb("O", [P, B, NC * NJ, E], BF16)

        w2 = up[:, :, :].rearrange("p g t -> p (g t)")[:, 0:E * F]

        base = sb("base", [P, E])
        place = sb("place", [P, NI * E])
        placef = sb("placef", [P, NI])
        placei = sb("placei", [P, 2, NI], U32)

        s8 = sb("s8", [P, 4, E])
        s8i = sb("s8i", [P, 2, E], I32)
        freei = sb("freei", [P, E], I32)
        ends = sb("ends", [P, NP, E])
        endw = sb("endw", [P, NP, E])
        eof = sb("eof", [P, 2, NP])
        eoi = sb("eoi", [P, NP], I32)
        rowi = sb("rowi", [P, NP], I32)

        pg = sb("pg", [P, RING, PAY])
        six = sb("six", [P, RING], U32)
        og = sb("og", [P, RING, D])
        gs = sb("gs", [P, 2, D])
        t1 = sb("t1", [P, 2, D])
        xT = sb("xT", [P, 2, P])
        ta = sb("ta", [P, 2])
        al = sb("al", [P, 2])
        w1c = sb("w1c", [P, 2, F])
        hTs = sb("hTs", [P, 2, F])

        psT = [ps("psT0"), ps("psT1")]
        psM = [ps(f"psM{g}") for g in range(G)]
        psA = ps("psA")
        psO = [ps("psO0"), ps("psO1")]
        psH, psY = [[psM[0], psM[1]], [psM[2], psA]], [psO[0], psO[1]]

        s_small, s_wmod, s_wi, s_wg, s_wo = sem("small_in"), sem("wmod_in"), sem("wi_in"), sem("wg_in"), sem("wo_in")
        s_x = [sem(f"x{c}_in") for c in range(NC)]
        s_ew = sem("experts_in")
        s_id0, s_const, s_zero, s_iota = sem("ident_zeroed"), sem("ident"), sem("zeroed"), sem("iotas")
        s_modB, s_gab = sem("modB_copied"), sem("gates_bounded")
        s_cond, s_silu, s_siluB = sem("cond_tanh"), sem("silu"), sem("siluB")
        s_mod, s_modev = sem("mod_mm"), sem("mod_copied")
        s_prep, s_dexp, s_decay, s_wog, s_wgd = sem("prep"), sem("decay_exp"), sem("decay"), sem("wo_gated"), sem("wg_diag")
        s_st = [sem(f"ln{n}_stats") for n in range(3)]
        s_mv = [sem(f"ln{n}_mean_var") for n in range(3)]
        s_ve = [sem(f"ln{n}_var_eps") for n in range(3)]
        s_rs = [sem(f"ln{n}_rstd") for n in range(3)]
        s_n1, s_xt, s_hT = sem("n1"), sem("x_turned"), sem("hT")
        s_mm, s_ev = sem("proj_mm"), sem("proj_read")
        s_up, s_conv, s_a, s_sq = sem("u_copied"), sem("conv"), sem("alpha"), sem("alpha_sq")
        s_y, s_beta = sem("one_less_sq"), sem("beta")
        s_v, s_xin, s_scan, s_carry, s_g = sem("gated_beta"), sem("rec_in"), sem("scan"), sem("carry"), sem("gelu_h")
        s_rank, s_place, s_dest, s_ids = sem("ranks_mm"), sem("place_steps"), sem("destinations"), sem("token_numbers")
        s_op, s_x1, s_n2, s_h2m, s_h2 = sem("wo_mm"), sem("x1"), sem("n2"), sem("h2_scaled"), sem("h2")
        s_rm, s_r, s_xn = sem("gb_h2"), sem("resid"), sem("xn")
        s_h2p, s_h2T, s_aff, s_am, s_ar = sem("h2_turned"), sem("h2T"), sem("aff_mm"), sem("aff_max"), sem("aff_read")
        s_rt, s_O, s_row = sem("route_steps"), sem("onehot"), [sem(f"rows_written{h}") for h in range(2)]
        s_dummy, s_free = sem("empty_pages_written"), sem("free_rows")
        s_tab, s_tabs = sem("table_steps"), sem("tables")
        s_passed = [sem(f"{e}_passed") for e in ("dve", "pool", "sp")]
        s_six = sem("scatter_index")
        s_gat = [sem(f"gathered{q}") for q in range(RING)]
        s_sct = [sem(f"scattered{q}") for q in range(RING)]
        s_pt, s_pxT, s_p1, s_p2 = sem("page_turned"), sem("page_xT"), sem("page_mm1"), sem("page_mm2")
        s_w1c = [sem("page_w1_act"), sem("page_w1_dve")]
        s_h = [sem("page_h_act"), sem("page_h_dve")]
        s_al, s_t1 = [sem(f"page_alpha{h}") for h in range(2)], [sem(f"page_y{h}") for h in range(2)]
        s_ta, s_gs, s_t2, s_o = sem("page_tanh"), sem("page_gate"), sem("page_yg"), sem("page_out")

        ORDER = ("u0", "u1", "u2", "gate0", "forget0", "gate1", "forget1", "gate2", "forget2", "input0", "input1",
                 "input2")
        INS = ("u0", "u1", "u2", "gate0", "gate1", "gate2")
        GATES = ("forget0", "forget1", "forget2", "input0", "input1", "input2")

        def nth_in(c, k):
            return k if c == 0 else NM * c - 6 + ORDER.index(INS[k])

        def nth_gate(c, k):
            return NM * c + 6 + (ORDER.index(GATES[k]) if c + 1 < NC else k)

        def tm(s):
            return bass.ds(s * TC, TC)

        def table(eng, tab, k, n, top):
            return nc.values_load_multi_w_load_instructions(
                tab[0:1, bass.ds(k, n)], engines=[eng.engine], min_val=0, max_val=top,
                skip_runtime_bounds_check_because="the counts that the tables are made of add up to the tokens")[1]

        def experts(eng, k, n):
            return table(eng, eoi, k, n, E - 1)

        def modulate(g, c):
            for b in range(B):
                ge(g, s_n2, NI * c + NJ * (b + 1))
                hb = h2[:, c % 2, b * NJ:(b + 1) * NJ, :]
                g.tensor_tensor(hb, hb, bc(cbB[:, b, :], NJ), ALU.mult).then_inc(s_h2m, 1)

        def gated(g, c):
            ge(g, s_scan, 3 * c + 3)
            ge(g, s_op, 2 * c)
            g.tensor_tensor(gh[:, :, :], gg[:, :, tm(c)], hh[:, :, :], ALU.mult).then_inc(s_g, 1)

        def bc(ap, n):
            return ap.unsqueeze(1).to_broadcast([P, n, ap.shape[-1]])

        block = ctx.enter_context(nc.Block())

        @block.sync
        def _(sp):
            sp.dma_start(small[:, :], small_d).then_inc(s_small, 16)
            sp.dma_start(wmod[:, :], wmod_d).then_inc(s_wmod, 16)

            def load_x(c):
                for b in range(B):
                    sp.dma_start(xs[:, c, b * NJ:(b + 1) * NJ, :],
                                 x_d[b, c * TC:(c + 1) * TC, :].rearrange("(j p) d -> p j d", p=P)).then_inc(s_x[c], 16)

            load_x(0)
            sp.dma_start(WiT[:, :], WiT_d).then_inc(s_wi, 16)
            sp.dma_start(WgA[:, :], WgT_d[0:P, :]).then_inc(s_wg, 16)
            for b in range(B):
                sp.dma_start(WgH[b * HH:(b + 1) * HH, :], WgT_d[P:HID, :]).then_inc(s_wg, 16)
            sp.dma_start(WoA[:, :], WoT_d[0:P, :]).then_inc(s_wo, 16)
            for b in range(B):
                sp.dma_start(WoH[b * HH:(b + 1) * HH, :], WoT_d[P:HID, :]).then_inc(s_wo, 16)
            for c in range(1, NC):
                load_x(c)
            sp.dma_start(w1[:, :].rearrange("d (e f) -> d e f", e=E), w1_d.rearrange("e d f -> d e f")).then_inc(s_ew, 16)
            sp.dma_start(b2B[:, :], b2_d.partition_broadcast(P)).then_inc(s_ew, 16)

            sp.wait_ge(s_iota, 2)
            for k in range(E - 1):
                sp.dma_start(rows_d[E * REG + k * P:E * REG + (k + 1) * P, :], empty[:, :]).then_inc(s_dummy, 16)
            sp.wait_ge(s_conv, 9 * NC)
            sp.dma_start(w2.rearrange("p (n d) -> p n d", d=D),
                         w2_d.rearrange("e (j p) d -> p (e j) d", p=P)).then_inc(s_ew, 16)
            sp.wait_ge(s_free, 1)
            free = table(sp, freei, 0, E // 2, E * REG - P)
            for e in range(E // 2):
                sp.dma_start(rows_d[bass.ds(free[e], P), :], empty[:, :]).then_inc(s_dummy, 16)

            def fetch(k, q, row):
                sp.dma_start(pg[:, q, :], rows_d[bass.ds(row, P), :]).then_inc(s_gat[q], 16)

            sp.wait_ge(s_dummy, 16 * (2 * E - 1))
            for h in range(2):
                sp.wait_ge(s_row[h], 16 * NT // 2)
            sp.wait_ge(s_tabs, 2)
            starts = table(sp, rowi, 0, RING, E * REG + (E - 2) * P)
            for k in range(RING):
                fetch(k, k, starts[k])
            with sp.Fori(1, NP // RING) as lap:
                starts = table(sp, rowi, lap * RING, RING, E * REG + (E - 2) * P)
                for q in range(RING):
                    ge_apart(sp, s_o, lap * RING - RING + q + 1, s_passed[2])
                    ge_apart(sp, s_six, lap * RING - RING + q + 1, s_passed[2])
                    fetch(lap * RING + q, q, starts[q])
            first = NP // RING * RING
            starts = table(sp, rowi, first, NP % RING, E * REG + (E - 2) * P)
            for k in range(first, NP):
                sp.wait_ge(s_o, k - RING + 1)
                sp.wait_ge(s_six, k - RING + 1)
                fetch(k, k % RING, starts[k - first])

        @block.tensor
        def _(pe):
            pe.wait_ge(s_wmod, 16)
            pe.wait_ge(s_silu, 2)
            for n in range(2):
                mm = pe.matmul(psA[:, 2 * n:2 * n + 2], wmod[:, n * D:(n + 1) * D], silu[:, :], start=True, stop=True)
            mm.then_inc(s_mod, 1)
            pe.wait_ge(s_siluB, B)
            for b in range(B):
                pe.matmul(psO[b][:, :], siluB[:, b, :], wmod[:, 2 * D:6 * D], start=True, stop=True).then_inc(s_mod, 1)

            def turn_x(c):
                for b in range(B):
                    ge(pe, s_h2T, 2 * (c - 5) + b + 1)
                    ge(pe, s_n1, NI * c + NJ * (b + 1))
                    for j in range(NJ):
                        mm = pe.transpose(psT[b][:, j * P:(j + 1) * P], n1[:, b * NJ + j, :], ident[:, :])
                    mm.then_inc(s_xt, 1)

            def project(n, parts):
                ge(pe, s_ev, n - G + 1)
                for out, lhsT, rhs, start, stop in parts:
                    mm = pe.matmul(out, lhsT, rhs, start=start, stop=stop, skip_group_check=True)
                mm.then_inc(s_mm, 1)

            def project_in(c, k):
                n = nth_in(c, k)
                ring = psM[n % G]
                ch = HID * (1 - k // 3)
                g = k % 3
                if g < 2:
                    project(n, [(ring[:, 0:TC], WiT[:, ch:ch + P], hT[:, g, :], True, True)])
                else:
                    project(n, [(ring[b * HH:(b + 1) * HH, 0:TC], WiT[:, ch + P:ch + HID], hT[:, b, :], True, True)
                                for b in range(B)])

            def project_gate(c, k):
                n = nth_gate(c, k)
                ring = psM[n % G]
                o = HID * (k // 3)
                g = k % 3
                if g < 2:
                    half = slice(g * HH, (g + 1) * HH)
                    project(n, [(ring[:, 0:TC], WgA[:, o:o + P], uc[:, c % 3, g, :], True, False),
                                (ring[:, 0:TC], WgH[half, o:o + P], uc[half, c % 3, 2, :], False, True)])
                else:
                    project(n, [(ring[:, 0:TC], WgD[:, k // 3, :], uc[:, c % 3, 2, :], True, False)]
                            + [(ring[b * HH:(b + 1) * HH, 0:TC], WgA[:, o + P:o + HID], uc[:, c % 3, b, :], False, True)
                               for b in range(B)])

            def project_out(c):
                ge(pe, s_g, c + 1)
                ge(pe, s_x1, 2 * c)
                for b in range(B):
                    half = slice(b * HH, (b + 1) * HH)
                    for j in range(NJ):
                        out = psO[b][:, j * D:(j + 1) * D]
                        pe.matmul(out, gh[:, b, j * P:(j + 1) * P], WoAg[:, b, :], start=True, stop=False)
                        mm = pe.matmul(out, gh[half, 2, j * P:(j + 1) * P], WoHg[half, :], start=False, stop=True)
                    mm.then_inc(s_op, 1)

            def turn_h2(c):
                for b in range(B):
                    ge(pe, s_h2, 2 * c + b + 1)
                    ge(pe, s_hT, 2 * min(c + 4, NC - 1) + b + 1)
                    for j in range(NJ):
                        mm = pe.transpose(psT[b][:, j * P:(j + 1) * P], h2[:, c % 2, b * NJ + j, :], ident[:, :])
                    mm.then_inc(s_h2p, 1)

            def affinities(c):
                ge(pe, s_ar, c)
                ge(pe, s_place, 4 * (c - 1) + 2)
                for b in range(B):
                    ge(pe, s_h2T, 2 * c + b + 1)
                    for j in range(NJ):
                        i = b * NJ + j
                        mm = pe.matmul(psA[:, i * E:(i + 1) * E], h2T[:, i, :], small[:, CENT:CENT + E],
                                       start=True, stop=True)
                mm.then_inc(s_aff, 1)

            def ranks(c):
                ge(pe, s_O, 2 * c + 2)
                ge(pe, s_place, 4 * c)
                ge(pe, s_ar, c + 1)
                onehot = lambda i: O[:, i // NJ, c * NJ + i % NJ, :]
                for i in range(NI + 1):
                    out = psA[:, (NI + i) * E:(NI + i + 1) * E]
                    for n in range(i):
                        mm = pe.matmul(out, ones[:, :], onehot(n), start=(n == 0), stop=(n == NI - 1))
                    if i < NI:
                        mm = pe.matmul(out, below[:, :], onehot(i), start=(i == 0), stop=True)
                mm.then_inc(s_rank, 1)

            pe.wait_ge(s_const, 1)
            for s in range(-2, NC + 1):
                if s == -1:
                    pe.wait_ge(s_wi, 16)
                if s == 0:
                    pe.wait_ge(s_wg, 48)
                    pe.wait_ge(s_wgd, 4)
                for name in ORDER:
                    if name in INS and 0 <= s + 1 < NC:
                        ge(pe, s_hT, 2 * (s + 1) + 2)
                        project_in(s + 1, INS.index(name))
                    if name in GATES and 0 <= s < NC:
                        ge(pe, s_conv, 9 * s + 9)
                        project_gate(s, GATES.index(name))
                    if name == "gate0" and s >= 3:
                        affinities(s - 3)
                if s >= 3:
                    if s == 3:
                        pe.wait_ge(s_iota, 2)
                    ranks(s - 3)
                if s + 2 < NC:
                    turn_x(s + 2)
                if 0 <= s - 1 < NC:
                    if s == 1:
                        pe.wait_ge(s_wog, 3)
                    project_out(s - 1)
                if 0 <= s - 2 < NC:
                    turn_h2(s - 2)
            affinities(NC - 2)
            ranks(NC - 2)
            turn_h2(NC - 1)
            affinities(NC - 1)
            ranks(NC - 1)

            def turn_page(k, q, lap):
                pe.wait_ge(s_gat[q], 16 * (lap + 1))
                ge(pe, s_pxT, k - 1)
                pe.transpose(psT[q % 2][:, 0:P], pg[:, q, 0:D], ident[:, :]).then_inc(s_pt, 1)

            def up_page(k, q):
                pe.wait_ge(s_pxT, k + 1)
                for half in range(2):
                    pe.wait_ge(s_w1c[half], k + 1)
                    for j in range(FJ // 2):
                        f = (half * FJ // 2 + j) * P
                        mm = pe.matmul(psH[q % 2][half][:, j * P:(j + 1) * P], w1c[:, q % 2, f:f + P],
                                       xT[:, q % 2, :], start=True, stop=True)
                    mm.then_inc(s_p1, 1)

            def down_page(k, q, lap, e):
                ge(pe, s_t1[q % 2], HALF * lap + q // 2)
                for j in range(FJ):
                    if j % (FJ // 2) == 0:
                        pe.wait_ge(s_h[2 * j // FJ], k + 1)
                    mm = pe.matmul(psY[q % 2][:, 0:D], hTs[:, q % 2, j * P:(j + 1) * P],
                                   w2[:, bass.ds(e * F + j * D, D)], start=(j == 0), stop=(j == FJ - 1))
                mm.then_inc(s_p2, 1)

            turn_page(0, 0, 0)
            turn_page(1, 1, 0)
            up_page(0, 0)

            def page(k, q, lap, es):
                if not isinstance(k, int) or k + 1 < NP:
                    up_page(k + 1, q + 1)
                if not isinstance(k, int) or k + 2 < NP:
                    turn_page(k + 2, (q + 2) % RING, lap + (q + 2) // RING)
                down_page(k, q, lap, es[q])

            pe.wait_ge(s_ew, 48)
            pe.wait_ge(s_tabs, 1)
            es = experts(pe, 0, RING)
            for k in range(RING):
                page(k, k, 0, es)
            with pe.Fori(1, NP // RING) as lap:
                es = experts(pe, lap * RING, RING)
                for q in range(RING):
                    page(lap * RING + q, q, lap, es)
            es = experts(pe, NP // RING * RING, NP % RING)
            for k in range(NP // RING * RING, NP):
                page(k, k % RING, k // RING, es)

        @block.scalar
        def _(act):
            act.wait_ge(s_small, 16)
            act.activation(silu[:, :], small[:, COND:COND + B], ACT.Tanh, scale=0.5).then_inc(s_cond, 1)
            act.wait_ge(s_prep, 3)
            act.activation(decay[:, 1, :], decay[:, 0, :], ACT.Exp).then_inc(s_dexp, 1)

            def scale_hT(c):
                for b in range(B):
                    ge(act, s_xt, 2 * c + b + 1)
                    if c:
                        ge(act, s_mm, nth_in(c - 1, 5) + 1)
                    act.activation(hT[:, b, :], psT[b][:, 0:TC], ACT.Identity, bias=modT[:, b:b + 1],
                                   scale=modT[:, 2 + b:3 + b]).then_inc(s_hT, 1)

            def read_in(c, k):
                n = nth_in(c, k)
                g = k % 3
                ge(act, s_mm, n + 1)
                if k < 3:
                    act.activation(up[:, g, bass.ds(c * TC + 3, TC)], psM[n % G][:, 0:TC], ACT.Copy).then_inc(s_up, 1)
                    if g == 0:
                        ge(act, s_xin, c - 2)
                    act.activation(uc[:, c % 3, g, :], psM[n % G][:, 0:TC], ACT.Identity,
                                   bias=small[:, CONV_B + g:CONV_B + g + 1],
                                   scale=small[:, CONV_W + 9 + g:CONV_W + 10 + g]).then_inc(s_ev, 1)
                else:
                    act.activation(gg[:, g, tm(c)], psM[n % G][:, 0:TC], ACT.Gelu).then_inc(s_ev, 1)

            def read_gate(c, k):
                n = nth_gate(c, k)
                ge(act, s_mm, n + 1)
                if k == 3:
                    ge(act, s_v, c)
                act.activation((tf, ti)[k // 3][:, k % 3, :], psM[n % G][:, 0:TC], ACT.Tanh,
                               bias=bgh[:, k:k + 1], scale=0.5).then_inc(s_ev, 1)

            def alpha(c):
                ge(act, s_scan, 3 * c)
                for g in range(G):
                    ge(act, s_ev, nth_gate(c, g) + 1)
                    act.activation(av[:, g, :], tf[:, g, :], ACT.Exp, bias=decay[:, 4, g:g + 1],
                                   scale=decay[:, 4, g:g + 1]).then_inc(s_a, 1)
                ge(act, s_a, 3 * c + 3)
                act.activation(tf[:, :, :], av[:, :, :], ACT.Square).then_inc(s_sq, 1)

            def beta(c):
                ge(act, s_y, c + 1)
                act.activation(bt[:, :, :], bt[:, :, :], ACT.Sqrt, bias=epsc[:, :]).then_inc(s_beta, 1)

            def copy_h2T(c):
                for b in range(B):
                    ge(act, s_h2p, 2 * c + b + 1)
                    ge(act, s_aff, c)
                    act.activation(h2T[:, b * NJ:(b + 1) * NJ, :].rearrange("p j t -> p (j t)"), psT[b][:, 0:TC],
                                   ACT.Copy).then_inc(s_h2T, 1)

            for s in range(-2, NC + 2):
                if s == -1:
                    act.wait_ge(s_zero, 1)
                if s == 0:
                    act.wait_ge(s_prep, 5)
                for name in ORDER:
                    if name in INS and 0 <= s + 1 < NC:
                        read_in(s + 1, INS.index(name))
                    if name in GATES and 0 <= s < NC:
                        read_gate(s, GATES.index(name))
                if 0 <= s < NC:
                    if s == 0:
                        act.wait_ge(s_decay, 8)
                        act.wait_ge(s_iota, 1)
                    alpha(s)
                if s + 2 < NC:
                    if s < -1:
                        act.wait_ge(s_modev, 2)
                    scale_hT(s + 2)
                if s == -1:
                    for b in range(B):
                        act.wait_ge(s_mod, 2 + b)
                        act.activation(modB[:, b, :, :].rearrange("p n d -> p (n d)"), psO[b][:, :],
                                       ACT.Copy).then_inc(s_modB, 1)
                if 0 <= s < NC:
                    beta(s)
                if s >= 2:
                    copy_h2T(s - 2)

            def scale_page(k, q, e):
                if not isinstance(k, int) or k >= 2:
                    act.wait_ge(s_p1, 2 * k - 3)
                act.activation(w1c[:, q % 2, 0:F // 2], w1[:, bass.ds(e * F, F // 2)], ACT.Copy).then_inc(s_w1c[0], 1)
                act.wait_ge(s_pt, k + 1)
                ge(act, s_p1, 2 * k - 2)
                act.activation(xT[:, q % 2, :], psT[q % 2][:, 0:P], ACT.Identity, bias=small[:, bass.ds(LN_B + e, 1)],
                               scale=small[:, bass.ds(LN_G + e, 1)]).then_inc(s_pxT, 1)

            def page(k, q, lap, es):
                act.wait_ge(s_p1, 2 * k + 1)
                ge(act, s_p2, k - 1)
                for j in range(FJ // 2):
                    h = act.activation(hTs[:, q % 2, j * P:(j + 1) * P], psH[q % 2][0][:, j * P:(j + 1) * P], ACT.Relu,
                                       bias=small[:, bass.ds(es[q] * FJ + (B1 + j), 1)])
                h.then_inc(s_h[0], 1)
                if not isinstance(k, int) or k + 2 < NP:
                    scale_page(k + 2, q, es[q + 2])
                act.wait_ge(s_gat[q], 16 * (lap + 1))
                ge(act, s_al[q % 2], HALF * lap + q // 2)
                act.activation(ta[:, q % 2:q % 2 + 1], pg[:, q, 2 * D:2 * D + 1], ACT.Tanh, scale=0.5).then_inc(s_ta, 1)

            act.wait_ge(s_free, 1)
            free = table(act, freei, E // 2, E // 2, E * REG - P)
            for e in range(E // 2):
                act.dma_start(rows_d[bass.ds(free[e], P), :], empty[:, :]).then_inc(s_dummy, 16)
            act.wait_ge(s_tabs, 1)
            es = experts(act, 0, RING + 2)
            act.wait_ge(s_ew, 48)
            scale_page(0, 0, es[0])
            scale_page(1, 1, es[1])
            for k in range(RING):
                page(k, k, 0, es)
            with act.Fori(1, NP // RING) as lap:
                es = experts(act, lap * RING, RING + 2)
                for q in range(RING):
                    page(lap * RING + q, q, lap, es)
            es = experts(act, NP // RING * RING, NP % RING)
            for k in range(NP // RING * RING, NP):
                page(k, k % RING, k // RING, es)

        @block.vector
        def _(dve):
            v = dve
            steps = [0]

            def prep(ins):
                ins.then_inc(s_prep, 1)
                steps[0] += 1
                v.wait_ge(s_prep, steps[0])

            v.wait_ge(s_small, 16)
            prep(v.tensor_scalar(decay[:, 0, :], small[:, FORGET:FORGET + G], -1.0, None, ALU.mult))
            prep(v.tensor_tensor(decay[:, 3, :], small[:, FORGET:FORGET + G], decay[:, 0, :], ALU.max))
            prep(v.tensor_scalar(decay[:, 0, :], decay[:, 3, :], -1.0, None, ALU.mult))
            prep(v.tensor_scalar(bgh[:, :], small[:, BG_F:BG_F + 2 * G], 0.5, None, ALU.mult))
            prep(v.tensor_scalar(decay[:, 3, :], small[:, FORGET:FORGET + G], 0.0, -4.0, ALU.max, ALU.mult))
            v.wait_ge(s_cond, 1)
            v.scalar_tensor_tensor(out=silu[:, :], in0=silu[:, :], scalar=1.0, in1=small[:, COND:COND + B],
                                   op0=ALU.add, op1=ALU.mult).then_inc(s_silu, 1)
            v.wait_ge(s_silu, 1)
            v.tensor_scalar(silu[:, :], silu[:, :], 0.5, None, ALU.mult).then_inc(s_silu, 1)
            v.wait_ge(s_silu, 2)
            v.wait_ge(s_iota, 1)
            for b in range(B):
                v.tensor_scalar(siluB[:, b, :], zeros[:, :], 0.0, silu[:, b:b + 1], ALU.mult,
                                ALU.add).then_inc(s_siluB, 1)
            v.wait_ge(s_mod, 1)
            v.tensor_copy(modT[:, 0:2], psA[:, 0:2]).then_inc(s_modev, 1)
            v.tensor_scalar(modT[:, 2:4], psA[:, 2:4], 1.0, None, ALU.add).then_inc(s_modev, 1)

            def ln_stats(n, c, tile):
                for i in range(NI):
                    v.bn_stats(st[:, n, i, :], tile(i)).then_inc(s_st[n], 1)
                ge_apart(v, s_st[n], NI * c + NI, s_passed[0])
                for i in range(NI):
                    v.bn_aggr(mv[:, n, i, :], st[:, n, i, :]).then_inc(s_mv[n], 1)

            def ln_out(n, c, tile, out, done):
                ge(v, s_rs[n], c + 1)
                for i in range(NI):
                    v.tensor_scalar(out(i), tile(i), mv[:, n, i, 0:1], rs[:, n, i:i + 1], ALU.subtract,
                                    ALU.mult).then_inc(done, 1)

            def conv_ready(c):
                ge(v, s_ev, nth_in(c, 2) + 1)
                ge(v, s_up, 3 * c + 3)

            def conv_tap(c, n):
                for g in range(G):
                    ge(v, s_conv, 9 * c + 3 * n + g - 5)
                    w = CONV_W + 3 * (3 - n) + g
                    v.scalar_tensor_tensor(out=uc[:, c % 3, g, :], in0=up[:, g, bass.ds(c * TC + 3 - n, TC)],
                                           scalar=small[:, w:w + 1], in1=uc[:, c % 3, g, :], op0=ALU.mult,
                                           op1=ALU.add).then_inc(s_conv, 1)

            def residual(c):
                for b in range(B):
                    ge(v, s_op, 2 * c + b + 1)
                    xb = xs[:, c, b * NJ:(b + 1) * NJ, :].rearrange("p j d -> p (j d)")
                    v.tensor_tensor(xb, xb, psO[b][:, 0:NJ * D], ALU.add).then_inc(s_x1, 1)
                v.wait_ge(s_x1, 2 * c + 2)

            def modulated(c):
                ge(v, s_h2p, 2 * c - 2)
                ge(v, s_rm, 2 * c - 2)
                ge(v, s_xn, NI * (c - 1))
                ln_out(1, c, lambda i: xs[:, c, i, :], lambda i: h2[:, c % 2, i, :], s_n2)

            def shift(c):
                for b in range(B):
                    ge(v, s_h2m, 2 * c + b + 1)
                    hb = h2[:, c % 2, b * NJ:(b + 1) * NJ, :]
                    v.tensor_tensor(hb, hb, bc(sbB[:, b, :], NJ), ALU.add).then_inc(s_h2, 1)
                v.wait_ge(s_h2, 2 * c + 2)

            def rows(c):
                ge(v, s_row[c % 2], 16 * NI * (c // 2))
                ln_out(2, c, lambda i: h2[:, c % 2, i, :], lambda i: pay[:, c % 2, i, 0:D], s_xn)
                for b in range(B):
                    ge(v, s_rm, 2 * c + b + 1)
                    rb = pay[:, c % 2, b * NJ:(b + 1) * NJ, D:2 * D]
                    v.tensor_tensor(rb, rb, xs[:, c, b * NJ:(b + 1) * NJ, :], ALU.add).then_inc(s_r, 1)

            def gate_input(c):
                ge(v, s_beta, c + 1)
                v.scalar_tensor_tensor(out=vx[:, :, :], in0=ti[:, :, :], scalar=1.0, in1=bt[:, :, :],
                                       op0=ALU.add, op1=ALU.mult).then_inc(s_v, 1)

            def scan(c, g):
                if g == 0:
                    ge(v, s_xin, c + 1)
                    ge(v, s_g, c)
                    ge(v, s_carry, c)
                v.tensor_tensor_scan(hh[:, g, :], av[:, g, :], vx[:, g, :], hc[:, g:g + 1] if c else 0.0, ALU.mult,
                                     ALU.add).then_inc(s_scan, 1)

            def carry(c):
                ge(v, s_scan, 3 * c + 3)
                v.tensor_copy(hc[:, :], hh[:, :, TC - 1]).then_inc(s_carry, 1)

            aff = psA[:, 0:NI * E].rearrange("p (i e) -> p i e", e=E)

            def largest(c):
                ge(v, s_aff, c + 1)
                v.tensor_reduce(am[:, :], aff, AX.X, ALU.max).then_inc(s_am, 1)

            def equals(c):
                ge(v, s_am, c + 1)
                v.tensor_tensor(oh[:, 0, :, :], aff, am[:, :].unsqueeze(2).to_broadcast([P, NI, E]),
                                ALU.is_equal).then_inc(s_ar, 1)
                ge(v, s_row[c % 2], 16 * NI * (c // 2))
                v.tensor_copy(pay[:, c % 2, :, 2 * D], am[:, :]).then_inc(s_rt, 1)

            def numbers(c):
                ge(v, s_ar, c + 1)
                v.tensor_tensor(oh[:, 1, :, :], oh[:, 0, :, :], bc(iotaE[:, :], NI), ALU.mult).then_inc(s_rt, 1)

            def first(c):
                ge(v, s_rt, 3 * c + 2)
                v.tensor_reduce(em[:, :], oh[:, 1, :, :], AX.X, ALU.min).then_inc(s_rt, 1)

            def onehot(c):
                ge(v, s_rt, 3 * c + 3)
                for b in range(B):
                    v.tensor_tensor(O[:, b, bass.ds(c * NJ, NJ), :], bc(iotaE[:, :], NJ),
                                    em[:, b * NJ:(b + 1) * NJ].unsqueeze(2).to_broadcast([P, NJ, E]),
                                    ALU.is_equal).then_inc(s_O, 1)

            def gates_of_modulation():
                v.wait_ge(s_gab, 11)
                prep(v.tensor_tensor(gbdiff[:, :], gbB[:, 1, :], gbB[:, 0, :], ALU.subtract))
                v.wait_ge(s_wo, 48)
                v.scalar_tensor_tensor(out=WoAg[:, :, :], in0=gaB[:, :, :], scalar=0.5, in1=bc(WoA[:, :], B),
                                       op0=ALU.mult, op1=ALU.mult).then_inc(s_wog, 1)
                for b in range(B):
                    half = slice(b * HH, (b + 1) * HH)
                    v.scalar_tensor_tensor(out=WoHg[half, :], in0=WoH[half, :], scalar=0.5, in1=gaB[half, b, :],
                                           op0=ALU.mult, op1=ALU.mult).then_inc(s_wog, 1)

            def split_weights():
                v.wait_ge(s_wg, 48)
                v.wait_ge(s_zero, 1)
                for n in range(2):
                    o = HID * n + P
                    for b in range(B):
                        half = slice(b * HH, (b + 1) * HH)
                        v.tensor_copy(WgD[half, n, half], WgH[half, o:o + HH]).then_inc(s_wgd, 1)
            def decays():
                v.wait_ge(s_dexp, 1)
                z, s, s2, acc = decay[:, 1, :], decay[:, 0, :], decay[:, 2, :], decay[:, 4, :]
                prep(v.tensor_scalar(s2, z, 2.0, None, ALU.add))
                prep(v.reciprocal(s2, s2))
                prep(v.tensor_tensor(s, z, s2, ALU.mult))
                prep(v.tensor_tensor(s2, s, s, ALU.mult))
                prep(v.tensor_scalar(acc, s2, 1.0 / 17, 1.0 / 15, ALU.mult, ALU.add))
                done = 0
                for n in (13, 11, 9, 7, 5, 3, 1):
                    v.tensor_tensor(acc, acc, s2, ALU.mult).then_inc(s_decay, 1)
                    done += 1
                    v.wait_ge(s_decay, done)
                    prep(v.tensor_scalar(acc, acc, 1.0 / n, None, ALU.add))
                prep(v.tensor_tensor(acc, acc, s, ALU.mult))
                v.scalar_tensor_tensor(out=acc, in0=acc, scalar=-8.0, in1=decay[:, 3, :], op0=ALU.mult,
                                       op1=ALU.add).then_inc(s_decay, 1)

            def places(c):
                ge(v, s_rank, c + 1)
                by_e = lambda a: a.rearrange("p (i e) -> p i e", e=E)
                v.tensor_tensor(by_e(place[:, :]), by_e(psA[:, NI * E:2 * NI * E]), bc(base[:, :], NI),
                                ALU.add).then_inc(s_place, 1)
                v.wait_ge(s_place, 4 * c + 1)
                v.tensor_tensor(base[:, :], base[:, :], psA[:, 2 * NI * E:(2 * NI + 1) * E], ALU.add).then_inc(s_place, 1)
                by_t = place[:, :].rearrange("p (b j e) -> p b j e", b=B, e=E)
                v.tensor_tensor(by_t, by_t, O[:, :, bass.ds(c * NJ, NJ), :], ALU.mult).then_inc(s_place, 1)
                v.wait_ge(s_place, 4 * c + 3)
                v.tensor_reduce(placef[:, :], by_e(place[:, :]), AX.X, ALU.add).then_inc(s_place, 1)
                v.wait_ge(s_place, 4 * c + 4)
                ge(v, s_row[c % 2], 16 * NI * (c // 2))
                v.tensor_copy(placei[:, c % 2, :], placef[:, :]).then_inc(s_dest, 1)

            for s in range(-2, NC + 1):
                ahead = lambda i: xs[:, s + 2, i, :]
                if 0 <= s - 1 < NC:
                    gate_input(s - 1)
                if 0 <= s - 2 < NC:
                    modulated(s - 2)
                if s + 2 < NC:
                    v.wait_ge(s_x[s + 2], 32)
                    ln_stats(0, s + 2, ahead)
                    if s == -1:
                        ge(v, s_xt, 2 * (s + 2))
                        ln_out(0, s + 2, ahead, lambda i: n1[:, i, :], s_n1)
                if s + 1 < NC:
                    if s >= -1:
                        conv_ready(s + 1)
                        conv_tap(s + 1, 1)
                if s >= 3:
                    if s == 3:
                        v.wait_ge(s_iota, 2)
                    largest(s - 3)
                if -1 <= s and s + 1 < NC:
                    conv_tap(s + 1, 2)
                if s >= 3:
                    equals(s - 3)
                if -1 <= s and s + 1 < NC:
                    conv_tap(s + 1, 3)
                if s >= 3:
                    numbers(s - 3)
                if s >= 1:
                    scan(s - 1, 0)
                if s >= 3:
                    first(s - 3)
                if s >= 1:
                    scan(s - 1, 1)
                if s >= 3:
                    onehot(s - 3)
                if s >= 1:
                    scan(s - 1, 2)
                    carry(s - 1)
                    if s == NC:
                        gated(v, s - 1)
                if s + 2 < NC and s != -1:
                    ge(v, s_xt, 2 * (s + 2))
                    ln_out(0, s + 2, ahead, lambda i: n1[:, i, :], s_n1)
                if 0 <= s - 2 < NC:
                    shift(s - 2)
                    ln_stats(2, s - 2, lambda i: h2[:, s % 2, i, :])
                if s >= 3:
                    places(s - 3)
                if 0 <= s - 1 < NC:
                    residual(s - 1)
                    ln_stats(1, s - 1, lambda i: xs[:, s - 1, i, :])
                if 0 <= s - 2 < NC - 2:
                    rows(s - 2)
                if s == -2:
                    split_weights()
                if s == -1:
                    decays()
                if s == 0:
                    gates_of_modulation()
            modulated(NC - 1)
            modulate(v, NC - 1)
            rows(NC - 2)
            for c in (NC - 2, NC - 1):
                largest(c)
                equals(c)
                numbers(c)
                first(c)
                onehot(c)
                places(c)
                if c == NC - 2:
                    shift(NC - 1)
                    ln_stats(2, NC - 1, lambda i: h2[:, (NC - 1) % 2, i, :])
            v.wait_ge(s_place, 4 * NC)
            v.tensor_copy(freei[:, :], base[:, :]).then_inc(s_free, 1)
            rows(NC - 1)

            tb = [0]

            def tab(ins):
                ins.then_inc(s_tab, 1)
                tb[0] += 1
                v.wait_ge(s_tab, tb[0])

            pages, pend, wide = (s8[:, n, :] for n in range(3))
            tab(v.tensor_scalar(s8i[:, 0, :], base[:, :], float(P - 1), None, ALU.add))
            tab(v.tensor_scalar(s8i[:, 1, :], s8i[:, 0, :], 7, None, ALU.logical_shift_right))
            tab(v.tensor_copy(pages, s8i[:, 1, :]))
            tab(v.scalar_tensor_tensor(out=pages, in0=iotaE[:, :], scalar=-float(REG // P), in1=pages, op0=ALU.mult,
                                       op1=ALU.add))
            tab(v.tensor_scalar(pages, pages, -float(E * (REG // P)), None, ALU.add))
            tab(v.tensor_tensor_scan(pend, onesf[:, :], pages, 0.0, ALU.mult, ALU.add))
            tab(v.tensor_tensor(ends[:, :, :], iotaP[:, :].unsqueeze(2).to_broadcast([P, NP, E]),
                                pend.unsqueeze(1).to_broadcast([P, NP, E]), ALU.is_ge))
            tab(v.tensor_reduce(eof[:, 0, :], ends[:, :, :], AX.X, ALU.add))
            v.tensor_scalar(eoi[:, :], eof[:, 0, :], float(E - 1), None, ALU.min).then_inc(s_tabs, 1)
            tab(v.tensor_scalar(wide, pages, -float(P), float(REG), ALU.mult, ALU.add))
            tab(v.tensor_tensor(endw[:, :, :], ends[:, :, :], wide.unsqueeze(1).to_broadcast([P, NP, E]), ALU.mult))
            tab(v.tensor_reduce(eof[:, 1, :], endw[:, :, :], AX.X, ALU.add))
            v.scalar_tensor_tensor(out=rowi[:, :], in0=iotaP[:, :], scalar=float(P), in1=eof[:, 1, :], op0=ALU.mult,
                                   op1=ALU.add).then_inc(s_tabs, 1)

            def relu_h(k, q, e):
                v.wait_ge(s_p1, 2 * k + 2)
                ge(v, s_p2, k - 1)
                for j in range(FJ // 2, FJ):
                    n = j - FJ // 2
                    h = v.tensor_scalar(hTs[:, q % 2, j * P:(j + 1) * P], psH[q % 2][1][:, n * P:(n + 1) * P],
                                        small[:, bass.ds(e * FJ + (B1 + j), 1)], 0.0, ALU.add, ALU.max)
                h.then_inc(s_h[1], 1)

            def copy_w1(k, q, e):
                ge(v, s_p1, 2 * k - 2)
                v.tensor_copy(w1c[:, q % 2, F // 2:F], w1[:, bass.ds(e * F + F // 2, F // 2)]).then_inc(s_w1c[1], 1)

            def page(k, q, lap, es):
                if not isinstance(k, int) or k + 1 < NP:
                    relu_h(k + 1, q + 1, es[q + 1])
                if not isinstance(k, int) or k + 2 < NP:
                    copy_w1(k + 2, q, es[q + 2])
                two = q % 2
                v.wait_ge(s_gat[q], 16 * (lap + 1))
                v.scalar_tensor_tensor(out=gs[:, two, :], in0=gbdiff[:, :], scalar=pg[:, q, 2 * D + 2:2 * D + 3],
                                       in1=gbB[:, 0, :], op0=ALU.mult, op1=ALU.add).then_inc(s_gs, 1)
                v.wait_ge(s_ta, k + 1)
                v.tensor_scalar(al[:, two:two + 1], ta[:, two:two + 1], 1.0, 0.5, ALU.add, ALU.mult).then_inc(s_al[two], 1)
                e = es[q]
                v.wait_ge(s_p2, k + 1)
                v.tensor_tensor(t1[:, two, :], psY[two][:, 0:D], b2B[:, bass.ds(e * D, D)], ALU.add).then_inc(s_t1[two], 1)
                v.wait_ge(s_t1[two], HALF * lap + q // 2 + 1)
                v.wait_ge(s_gs, k + 1)
                v.wait_ge(s_al[two], HALF * lap + q // 2 + 1)
                v.scalar_tensor_tensor(out=t1[:, two, :], in0=t1[:, two, :], scalar=al[:, two:two + 1],
                                       in1=gs[:, two, :], op0=ALU.mult, op1=ALU.mult).then_inc(s_t2, 1)
                v.wait_ge(s_t2, k + 1)
                ge(v, s_sct[q], 16 * lap)
                v.tensor_tensor(og[:, q, :], t1[:, two, :], pg[:, q, D:2 * D], ALU.add).then_inc(s_o, 1)

            v.wait_ge(s_tabs, 1)
            v.wait_ge(s_ew, 48)
            es = experts(v, 0, RING + 2)
            for k in range(2):
                copy_w1(k, k, es[k])
            relu_h(0, 0, es[0])
            for k in range(RING):
                page(k, k, 0, es)
            with v.Fori(1, NP // RING) as lap:
                es = experts(v, lap * RING, RING + 2)
                for q in range(RING):
                    page(lap * RING + q, q, lap, es)
            es = experts(v, NP // RING * RING, NP % RING)
            for k in range(NP // RING * RING, NP):
                page(k, k % RING, k // RING, es)

        @block.gpsimd
        def _(pool):
            g = pool
            g.memset(ident[:, :], 0.0).then_inc(s_id0, 1)
            g.memset(below[:, :], 1.0)
            g.memset(up[:, :, 0:3], 0.0)
            g.memset(WgD[:, :, :], 0.0).then_inc(s_zero, 1)
            g.memset(ones[:, :], 1.0)
            g.memset(zeros[:, :], 0.0)
            g.memset(epsc[:, :], 1e-6)
            g.memset(mhalf[:, :], -0.5).then_inc(s_iota, 1)
            g.wait_ge(s_id0, 1)
            g.affine_select(out=ident[:, :], in_=ident[:, :], compare_op=ALU.not_equal, fill=1.0, base=0,
                            pattern=[[-1, P]], channel_multiplier=1).then_inc(s_const, 1)

            def rstd(n, c):
                ge_apart(g, s_mv[n], NI * c + NI, s_passed[1])
                g.tensor_scalar(ve[:, n, :], mv[:, n, :, 1], EPS, None, ALU.add).then_inc(s_ve[n], 1)
                ge(g, s_ve[n], c + 1)
                g.tensor_tensor(rs[:, n, :], ve[:, n, :], mhalf[:, :], ALU.pow).then_inc(s_rs[n], 1)

            def bound_gates():
                done = [0]

                def step(ins):
                    ins.then_inc(s_gab, 1)
                    done[0] += 1
                    g.wait_ge(s_gab, done[0])

                g.wait_ge(s_modB, 2)
                step(g.tensor_scalar(cbB, cbB, 1.0, None, ALU.add))
                for n, gate in enumerate((gaB, gbB)):
                    size, sign = mtmp[:, n, 0, :, :], mtmp[:, n, 1, :, :]
                    step(g.tensor_scalar(sign, gate, 0.0, 2.0, ALU.is_ge, ALU.mult))
                    step(g.tensor_scalar(sign, sign, -1.0, None, ALU.add))
                    step(g.tensor_tensor(size, sign, gate, ALU.mult))
                    step(g.tensor_scalar(size, size, 0.25, None, ALU.max))
                    step(g.tensor_tensor(gate, sign, size, ALU.mult))

            def gate_h2(c):
                rstd(2, c)
                ge(g, s_row[c % 2], 16 * NI * (c // 2))
                for b in range(B):
                    ge(g, s_h2, 2 * c + b + 1)
                    g.tensor_tensor(pay[:, c % 2, b * NJ:(b + 1) * NJ, D:2 * D], h2[:, c % 2, b * NJ:(b + 1) * NJ, :],
                                    bc(gbB[:, b, :], NJ), ALU.mult).then_inc(s_rm, 1)
                    g.iota(pay[:, c % 2, b * NJ:(b + 1) * NJ, 2 * D + 1], pattern=[[P, NJ]], base=b * T + c * TC,
                           channel_multiplier=1, allow_small_or_imprecise_dtypes=True).then_inc(s_ids, 1)

            def dispatch(c, tiles):
                ge(g, s_ids, 2 * c + 2)
                ge(g, s_xn, NI * c + NI)
                ge(g, s_r, 2 * c + 2)
                ge(g, s_rt, 3 * c + 1)
                ge(g, s_dest, c + 1)
                for i in tiles:
                    g.indirect_dma_start(out=rows_d, out_offset=bass.IndirectOffsetOnAxis(
                        ap=placei[:, c % 2, i:i + 1], axis=0), in_=pay[:, c % 2, i, :],
                        in_offset=None).then_inc(s_row[c % 2], 16)

            def one_less_square(c):
                ge(g, s_sq, c + 1)
                ge(g, s_v, c)
                g.tensor_scalar(bt[:, :, :], tf[:, :, :], -1.0, 1.0, ALU.mult, ALU.add).then_inc(s_y, 1)

            def rec_input(c):
                ge(g, s_v, c + 1)
                g.tensor_tensor(vx[:, :, :], vx[:, :, :], uc[:, c % 3, :, :], ALU.mult).then_inc(s_xin, 1)

            rstd(0, 0)
            g.wait_ge(s_zero, 1)
            g.affine_select(out=below[:, :], in_=below[:, :], compare_op=ALU.is_gt, fill=0.0, base=0,
                            pattern=[[1, P]], channel_multiplier=-1)
            g.memset(pay[:, :, :, 2 * D + 3], 0.0)
            for b in range(B):
                g.memset(pay[:, :, b * NJ:(b + 1) * NJ, 2 * D + 2], float(b))
            g.memset(empty[:, 0:2 * D + 1], 0.0)
            g.memset(empty[:, 2 * D + 2:PAY], 0.0)
            g.memset(empty[:, 2 * D + 1:2 * D + 2], float(2 * B * T))
            g.iota(iotaE[:, :], pattern=[[1, E]], base=-E, channel_multiplier=0, allow_small_or_imprecise_dtypes=True)
            g.iota(iotaP[:, :], pattern=[[1, NP]], base=0, channel_multiplier=0, allow_small_or_imprecise_dtypes=True)
            g.iota(base[:, :], pattern=[[REG, E]], base=0, channel_multiplier=0, allow_small_or_imprecise_dtypes=True)
            g.memset(onesf[:, :], 1.0).then_inc(s_iota, 1)
            for s in range(-1, NC + 1):
                if 0 <= s - 1 < NC:
                    rec_input(s - 1)
                if 0 <= s - 2 < NC:
                    modulate(g, s - 2)
                if s + 2 < NC:
                    rstd(0, s + 2)
                if s == -1:
                    bound_gates()
                if s >= 4:
                    dispatch(s - 4, range(0, NI - 1))
                if 0 <= s - 1 < NC - 1:
                    gated(g, s - 1)
                if s >= 4:
                    dispatch(s - 4, range(NI - 1, NI))
                if 0 <= s < NC:
                    one_less_square(s)
                if s == NC:
                    dispatch(NC - 3, range(NI))
                    rstd(1, s - 1)
                if 0 <= s - 2 < NC:
                    gate_h2(s - 2)
                if 0 <= s - 1 < NC and s < NC:
                    rstd(1, s - 1)
            dispatch(NC - 2, range(NI - 1))
            gate_h2(NC - 1)
            dispatch(NC - 2, range(NI - 1, NI))
            dispatch(NC - 1, range(NI))

            def scatter(k, q, lap):
                ge_apart(g, s_gat[q], 16 * (lap + 1), s_passed[1])
                ge_apart(g, s_sct[q], 16 * lap, s_passed[1])
                g.tensor_copy(six[:, q:q + 1], pg[:, q, 2 * D + 1:2 * D + 2]).then_inc(s_six, 1)
                g.wait_ge(s_six, k + 1)
                ge_apart(g, s_o, k + 1, s_passed[1])
                g.indirect_dma_start(out=out_d, out_offset=bass.IndirectOffsetOnAxis(ap=six[:, q:q + 1], axis=0),
                                     in_=og[:, q, :], in_offset=None, bounds_check=B * T - 1,
                                     oob_is_err=False).then_inc(s_sct[q], 16)

            for k in range(RING):
                scatter(k, k, 0)
            with g.Fori(1, NP // RING) as lap:
                for q in range(RING):
                    scatter(lap * RING + q, q, lap)
            for k in range(NP // RING * RING, NP):
                scatter(k, k % RING, k // RING)
            for q in range(RING):
                g.wait_ge(s_sct[q], 16 * len(range(q, NP, RING)))


def kernel(**inputs):
    import numpy as _np
    import concourse.bacc as _bacc
    from concourse.bass_utils import run_bass_kernel_spmd as _run

    a = {n: _np.asarray(v) for n, v in inputs.items()}

    def groups(v):
        return _np.stack([v[:P], v[:P], _np.concatenate([v[P:], v[P:]])], axis=1)

    H = a["L0_attn_Wg"].shape[1]
    bg = a["L0_attn_bg"]
    cw = a["L0_attn_conv_w"][:, 0, :]
    small = _np.concatenate(
        [groups(a["L0_attn_conv_b"]), groups(bg[:H]), groups(bg[H:]), groups(a["L0_attn_forget_base"])]
        + [groups(cw[:, k]) for k in range(cw.shape[1])]
        + [a["L0_ffn_ln_g"].T, a["L0_ffn_ln_b"].T, a["L0_c"].T, a["L0_ffn_centroids"].T,
           a["L0_ffn_b1"].reshape(-1, P).T], axis=1)
    arrays = {
        "x": a["L0_attn_x"], "WiT": a["L0_attn_Wi"].T, "WgT": a["L0_attn_Wg"].T, "WoT": a["L0_attn_Wo"].T,
        "small": small, "w1": a["L0_ffn_w1"], "w2": a["L0_ffn_w2"],
        "b2": a["L0_ffn_b2"].reshape(-1), "wmod": a["L0_wmod"],
    }
    nc = _bacc.Bacc("TRN2", target_bir_lowering=False, num_devices=1)
    arrays = {f"in_{n}": _np.ascontiguousarray(v) for n, v in arrays.items()}
    args = [nc.dram_tensor(n, v.shape, mybir.dt.from_np(v.dtype), kind="ExternalInput").ap() for n, v in arrays.items()]
    shape = a["L0_attn_x"].shape
    out = nc.dram_tensor("out", (shape[0] * shape[1], shape[2]), F32, kind="ExternalOutput").ap()
    adaln_block_kernel(nc, *args, out)
    r = _run(nc, [arrays], core_ids=[0])
    return r.results[0]["out"].reshape(shape)
```
